# Optimizing a Trainium2 kernel written in Bass

```python
import numpy as np
import jax
import jax.numpy as jnp

def _softmax(x, axis=-1):
    return jax.nn.softmax(x, axis=axis)

def _gelu(x):
    return jax.nn.gelu(x, approximate=True)

def _silu(x):
    return jax.nn.silu(x)

def _sigmoid(x):
    return jax.nn.sigmoid(x)

def _layernorm(x, axis=-1, eps=1e-05):
    m = jnp.mean(x, axis=axis, keepdims=True)
    v = jnp.var(x, axis=axis, keepdims=True)
    return (x - m) / jnp.sqrt(v + eps)

def _scatter_add(tgt, idx, src, axis=0):
    return tgt.at[idx].add(src)

def _segment_sum(src, seg, n):
    return jax.ops.segment_sum(src, seg, n)
kernel_name = 'mk_xattn_ffn_d1_seqx_r4_313192'

def setup_inputs(seed: int=0):
    np.random.seed(seed)
    _w = jnp.asarray

    def _rec_inputs():
        import jax
        import jax.numpy as jnp
        _rk = jax.random.key(seed)
        x = -0.0002928 + 1 * jax.random.normal(jax.random.fold_in(_rk, 1), (8, 512, 256), jnp.float32)
        _lenS = 512 - jax.random.randint(jax.random.fold_in(_rk, 7), (8,), 0, max(1, 512 // 4) + 1, jnp.int32)
        _lenS2 = 1024 - jax.random.randint(jax.random.fold_in(_rk, 8), (8,), 0, max(1, 1024 // 4) + 1, jnp.int32)
        _ctx_1024P = jax.random.normal(jax.random.fold_in(_rk, 11), (8, 16, 256), jnp.float32)
        _ctx_1024c = jax.random.dirichlet(jax.random.fold_in(_rk, 511), 0.3 * jnp.ones((16,), jnp.float32), (8, 1024))
        _ctx_1024t = jnp.einsum('bsk,bkd->bsd', _ctx_1024c, _ctx_1024P)
        _ctx_1024t = _ctx_1024t * jax.lax.rsqrt(jnp.mean(jnp.square(_ctx_1024t)) + 1e-12) * 0.953939
        ctx_1024 = -1.39393e-06 + 0.999914 * (_ctx_1024t + 0.3 * jax.random.normal(jax.random.fold_in(_rk, 611), (8, 1024, 256), jnp.float32))
        _validS = jnp.arange(512)[None, :] < _lenS[:, None]
        _validS2 = jnp.arange(1024)[None, :] < _lenS2[:, None]
        _causal = jnp.tril(jnp.ones((512, 512), dtype=bool))
        mask_BxSxS2_bk1 = jnp.broadcast_to(_validS2[:, None, :], (8, 512, 1024))
        return (x, ctx_1024, mask_BxSxS2_bk1)
    x, ctx_1024, mask_BxSxS2_bk1 = _rec_inputs()

    def _L0_xattn_setup():
        import jax, jax.numpy as jnp
        import numpy as np
        B, TQ, TK, D, H = (2, 512, 512, 256, 16)
        key = jax.random.key(seed)
        ks = jax.random.split(key, 8)
        s = 1.0 / np.sqrt(D)
        x_q = jax.random.normal(ks[0], (B, TQ, D), jnp.float32)
        x_k = jax.random.normal(ks[1], (B, TK, D), jnp.float32)
        x_v = jax.random.normal(ks[2], (B, TK, D), jnp.float32)
        causal = jnp.triu(jnp.ones((TQ, TK), jnp.bool_), k=1)
        attn_mask = jnp.broadcast_to(causal, (B, TQ, TK))
        Wq = jax.random.normal(ks[3], (D, D), jnp.float32) * s
        Wk = jax.random.normal(ks[4], (D, D), jnp.float32) * s
        Wv = jax.random.normal(ks[5], (D, D), jnp.float32) * s
        Wo = jax.random.normal(ks[6], (D, D), jnp.float32) * s
        z = jnp.zeros((D,), jnp.float32)
        return {'x_q': x_q, 'x_k': x_k, 'x_v': x_v, 'attn_mask': attn_mask, 'Wq': Wq, 'bq': z, 'Wk': Wk, 'bk': z, 'Wv': Wv, 'bv': z, 'Wo': Wo, 'bo': z, 'n_heads': H}
    _L0_xattn_all = _L0_xattn_setup()
    _L0_xattn_in = {k: v for k, v in _L0_xattn_all.items() if k in ('Wq', 'bq', 'Wk', 'bk', 'Wv', 'bv', 'Wo', 'bo')}
    del _L0_xattn_all

    def _L0_ffn_setup():
        import jax, jax.numpy as jnp
        import numpy as np
        D = 256
        E = 12
        HS = 2 * D
        HR = 3 * D
        TAU = 1.5

        def _geglu(h):
            a, g = jnp.split(h, 2, axis=-1)
            return a * jax.nn.gelu(g, approximate=False)
        key = jax.random.key(seed)
        ks = jax.random.split(key, 12)

        def xavier(k, shape):
            fan_in, fan_out = (shape[-2], shape[-1])
            lim = jnp.sqrt(6.0 / (fan_in + fan_out))
            return jax.random.uniform(k, shape, jnp.float32, -lim, lim)
        x = jax.random.normal(ks[0], (2, 256, D), jnp.float32)
        Ws1 = xavier(ks[1], (D, 2 * HS))
        bs1 = jnp.zeros((2 * HS,), jnp.float32)
        Ws2 = xavier(ks[2], (HS, D))
        bs2 = jnp.zeros((D,), jnp.float32)
        We1 = xavier(ks[3], (E, D, 2 * HR))
        be1 = jnp.zeros((E, 2 * HR), jnp.float32)
        We2 = xavier(ks[4], (E, HR, D))
        be2 = jnp.zeros((E, D), jnp.float32)
        Wr = xavier(ks[5], (D, E))
        br = jnp.zeros((E,), jnp.float32)
        return {'x': x, 'Ws1': Ws1, 'bs1': bs1, 'Ws2': Ws2, 'bs2': bs2, 'We1': We1, 'be1': be1, 'We2': We2, 'be2': be2, 'Wr': Wr, 'br': br}
    _L0_ffn_all = _L0_ffn_setup()
    _L0_ffn_in = {k: v for k, v in _L0_ffn_all.items() if k in ('Ws1', 'bs1', 'Ws2', 'bs2', 'We1', 'be1', 'We2', 'be2', 'Wr', 'br')}
    del _L0_ffn_all
    return {'x': x, 'ctx_1024': ctx_1024, 'mask_BxSxS2_bk1': mask_BxSxS2_bk1, 'L0_xattn_Wq': _L0_xattn_in['Wq'], 'L0_xattn_bq': _L0_xattn_in['bq'], 'L0_xattn_Wk': _L0_xattn_in['Wk'], 'L0_xattn_bk': _L0_xattn_in['bk'], 'L0_xattn_Wv': _L0_xattn_in['Wv'], 'L0_xattn_bv': _L0_xattn_in['bv'], 'L0_xattn_Wo': _L0_xattn_in['Wo'], 'L0_xattn_bo': _L0_xattn_in['bo'], 'L0_ffn_Ws1': _L0_ffn_in['Ws1'], 'L0_ffn_bs1': _L0_ffn_in['bs1'], 'L0_ffn_Ws2': _L0_ffn_in['Ws2'], 'L0_ffn_bs2': _L0_ffn_in['bs2'], 'L0_ffn_We1': _L0_ffn_in['We1'], 'L0_ffn_be1': _L0_ffn_in['be1'], 'L0_ffn_We2': _L0_ffn_in['We2'], 'L0_ffn_be2': _L0_ffn_in['be2'], 'L0_ffn_Wr': _L0_ffn_in['Wr'], 'L0_ffn_br': _L0_ffn_in['br']}

def reference(x, ctx_1024, mask_BxSxS2_bk1, L0_xattn_Wq, L0_xattn_bq, L0_xattn_Wk, L0_xattn_bk, L0_xattn_Wv, L0_xattn_bv, L0_xattn_Wo, L0_xattn_bo, L0_ffn_Ws1, L0_ffn_bs1, L0_ffn_Ws2, L0_ffn_bs2, L0_ffn_We1, L0_ffn_be1, L0_ffn_We2, L0_ffn_be2, L0_ffn_Wr, L0_ffn_br):
    import jax
    import jax.numpy as jnp

    def _L0_xattn_ref(x_q, x_k, x_v, attn_mask, Wq, bq, Wk, bk, Wv, bv, Wo, bo, n_heads):
        import jax, jax.numpy as jnp
        import numpy as np
        B, TQ, TK, D, H = (2, 512, 512, 256, 16)
        Bv, Tq, Dm = x_q.shape
        Tk = x_k.shape[1]
        dh = Dm // n_heads
        Q = (jnp.einsum('btd,od->bto', x_q, Wq) + bq).reshape(Bv, Tq, n_heads, dh).transpose(0, 2, 1, 3)
        K = (jnp.einsum('btd,od->bto', x_k, Wk) + bk).reshape(Bv, Tk, n_heads, dh).transpose(0, 2, 1, 3)
        V = (jnp.einsum('btd,od->bto', x_v, Wv) + bv).reshape(Bv, Tk, n_heads, dh).transpose(0, 2, 1, 3)
        scale = 1.0 / np.sqrt(dh).astype(np.float32)
        scores = jnp.einsum('bhqd,bhkd->bhqk', Q, K) * scale
        scores = jnp.where(attn_mask[:, None, :, :], -jnp.inf, scores)
        A = jax.nn.softmax(scores, axis=-1)
        out = jnp.einsum('bhqk,bhkd->bhqd', A, V)
        out = out.transpose(0, 2, 1, 3).reshape(Bv, Tq, Dm)
        return jnp.einsum('btd,od->bto', out, Wo) + bo

    def _L0_ffn_ref(x, Ws1, bs1, Ws2, bs2, We1, be1, We2, be2, Wr, br):
        import jax, jax.numpy as jnp
        import numpy as np
        D = 256
        E = 12
        HS = 2 * D
        HR = 3 * D
        TAU = 1.5

        def _geglu(h):
            a, g = jnp.split(h, 2, axis=-1)
            return a * jax.nn.gelu(g, approximate=False)
        B, T, Dm = x.shape
        xf = x.reshape(-1, Dm)
        ys = _geglu(xf @ Ws1 + bs1) @ Ws2 + bs2
        logits = (xf @ Wr + br) / TAU
        top_val, top_idx = jax.lax.top_k(logits, 2)
        top_w = jax.nn.softmax(top_val, axis=-1)
        onehot = jax.nn.one_hot(top_idx, E, dtype=x.dtype)
        w = jnp.einsum('nke,nk->ne', onehot, top_w)
        h = jnp.einsum('nd,edh->enh', xf, We1) + be1[:, None, :]
        act = _geglu(h)
        yE = jnp.einsum('enh,ehd->end', act, We2) + be2[:, None, :]
        yr = jnp.einsum('end,ne->nd', yE, w)
        return (ys + yr).reshape(B, T, Dm)
    x = x + _L0_xattn_ref(_layernorm(x, axis=-1), ctx_1024, ctx_1024, mask_BxSxS2_bk1, L0_xattn_Wq, L0_xattn_bq, L0_xattn_Wk, L0_xattn_bk, L0_xattn_Wv, L0_xattn_bv, L0_xattn_Wo, L0_xattn_bo, 16)
    x = x + _L0_ffn_ref(_layernorm(x, axis=-1), L0_ffn_Ws1, L0_ffn_bs1, L0_ffn_Ws2, L0_ffn_bs2, L0_ffn_We1, L0_ffn_be1, L0_ffn_We2, L0_ffn_be2, L0_ffn_Wr, L0_ffn_br)
    return x

_drawn_inputs = setup_inputs


def setup_inputs(seed=0):
    import zlib

    import numpy as np

    out = dict(_drawn_inputs(seed))
    spreads = {'L0_xattn_bq': (0.0, 0.1),
     'L0_xattn_bk': (0.0, 0.1),
     'L0_xattn_bv': (0.0, 0.1),
     'L0_xattn_bo': (0.0, 0.1),
     'L0_ffn_bs1': (0.0, 0.1),
     'L0_ffn_bs2': (0.0, 0.1),
     'L0_ffn_be1': (0.0, 0.1),
     'L0_ffn_be2': (0.0, 0.1),
     'L0_ffn_br': (0.0, 0.1)}
    factors = {}
    for name, (base, spread) in spreads.items():
        noise = np.random.default_rng([zlib.crc32(name.encode()), seed]).standard_normal(out[name].shape)
        drawn = base * np.exp(spread * noise) if base else spread * noise
        out[name] = jnp.asarray(drawn.astype(out[name].dtype))
    for name, factor in factors.items():
        out[name] = (out[name] * factor).astype(out[name].dtype)
    return out
```

```python
import concourse.bass as bass
from concourse import mybir
from contextlib import ExitStack

FP32, FP16, BF16 = mybir.dt.float32, mybir.dt.float16, mybir.dt.bfloat16
I32, U32, U8 = mybir.dt.int32, mybir.dt.uint32, mybir.dt.uint8
ALU, ACT, AX = mybir.AluOpType, mybir.ActivationFunctionType, mybir.AxisListType

P = 128
B, TQ, TK, D = 8, 512, 1024, 256
H, DH = 16, 16
QT = TQ // P
DT = D // P
N = B * TQ
NT = N // P
KC = 256
NPAIR = H // 2
PARTS = 4
GROUPS = H // 4
E, HS, HR = 12, 512, 768
TAU = 1.5
EPS = 1e-5
MASKED = -60000.0
MASK_ROWS = 14
NEG = -1e30


class Path:

    ONCE = ("cleared", "extras")
    ONLY_MASKED = ("mask_loaded", "mask_ready", "negm")

    def __init__(self, nc, ctx, name, chunks, buffers, masked, before=None):
        self.name, self.chunks, self.buffers, self.masked = name, chunks, buffers, masked
        c = len(chunks)
        self.nc_ = c
        self.per = dict(
            x_loaded=16, ctx_loaded=16 * c, res_loaded=16, mask_loaded=16, mask_ready=1,
            ln1_link=2, ve1=1, rstd1=1, xn_ready=1, xT_mm=2, xTh=2, xTl=2, q_mm=2, qf=2, qh=2, ql=2,
            cT_mm=c, cTh=c, cTl=c, k_mm=c, kf=c, kh=c, kl=c, v_mm=c, v_ready=c,
            qstk_w=32, qs_loaded=128, kstk_w=32 * c, kz_loaded=(96 if masked else 128) * c,
            s_mm=32 * c, max_done=32 * c, negm=1, mT_mm=1, mT_ready=1, m_saved=16, m_rows=32,
            st_mm=32 * c, exp_done=32 * c, pv_mm=8 * c, oT_ready=4, oX_mm=4, rec=4, on_ready=4,
            onT_mm=2, onTh=2, onTl=2, o_mm=2, res_ready=1, x1_done=2, ln2_link=2, ve2=1, rstd2=1,
            xn2_ready=1, xn2_saved=16, acc_done=1, x2T_mm=2, x2h=2, x2l=2, r_mm=1, rt_link=5,
            cleared=1, extras=16 * 2 * (buffers + max(buffers, c)))
        if before is None:
            self.passed = ctx.enter_context(nc.semaphore(f"{name}_passed"))
            self.sem = {n: ctx.enter_context(nc.semaphore(f"{name}_{n}")) for n in self.per}
            self.ahead = dict(self.per)
        else:
            self.passed, self.sem = before.passed, before.sem
            self.ahead = {n: before.ahead[n] + before.per[n] * (0 if n in self.ONLY_MASKED else 1 if n in self.ONCE else B)
                          for n in self.per}

    def start_ahead(self, eng):
        for n, s in self.sem.items():
            eng.sem_inc(s, self.ahead[n])

    def until(self, eng, name, count, alone=False):
        if isinstance(count, int) and count <= 0:
            return
        eng.wait_ge(self.sem[name], count + self.ahead[name])
        if alone and not isinstance(count, int):
            eng.sem_inc(self.passed, 1)

    def of(self, name, b, k):
        return b * self.per[name] + k


MISC = dict(oX0=0, oX1=1, oX2=0, mT=1, oX3=0, xT0=1, xT1=0, onT0=1, onT1=0, cT=1, O0=0, O1=1,
            Q0=0, Q1=1, K=0, V=1, x2T0=0, x2T1=1, R=0)


def attention(nc, path, io, keep, scratch):
    ctx = ExitStack()
    C, NB, general = path.nc_, path.buffers, path.masked
    sem, until, of, sem_per = path.sem, path.until, path.of, path.per

    def sb(name, shape, dt):
        return ctx.enter_context(nc.sbuf_tensor(f"{path.name}_{name}", shape, dt))

    xbuf = sb("xbuf", [P, QT, D], FP32)
    xres = sb("xres", [P, QT, D], FP32)
    xn = sb("xn", [P, QT, D], FP32)
    stats = sb("stats", [P, QT, 6], FP32)
    mv = sb("mv", [P, QT, 2], FP32)
    rstd = sb("rstd", [P, QT], FP32)
    xTh = sb("xTh", [P, DT, TQ], FP16)
    xTl = sb("xTl", [P, DT, TQ], FP16)
    qf = sb("qf", [P, DT, TQ], FP32)
    qh = sb("qh", [P, DT, TQ], FP16)
    ql = sb("ql", [P, DT, TQ], FP16)
    cbuf = sb("cbuf", [P, 2, D], FP32)
    cTh = sb("cTh", [P, DT, KC], FP16)
    cTl = sb("cTl", [P, DT, KC], FP16)
    kf = sb("kf", [P, DT, KC], FP32)
    kh = sb("kh", [P, DT, KC], FP16)
    kl = sb("kl", [P, DT, KC], FP16)
    nk = max(NB, C)
    Qs = [sb(f"Qs{u}", [P, NPAIR, TQ], FP16) for u in range(NB)]
    Kz = [sb(f"Kz{u}", [P, NPAIR, 2, KC], FP16) for u in range(nk)]
    V = [sb(f"V{u}", [P, 2, H, 32], FP32) for u in range(nk)]
    NPT = 4 if general else 8
    PT = sb("PT", [P, NPT, TQ], FP32)
    mx = sb("mx", [P, QT, H, C], FP32)
    negm = sb("negm", [P, QT, H], FP32)
    mT16 = sb("mT16", [H, TQ], FP16)
    oT = sb("oT", [P, 2, TQ], FP32)
    rec = sb("rec", [P, QT, 4], FP32)
    if general:
        on = qf[:].rearrange("p o (u d) -> p (o u) d", d=D)
    else:
        on = sb("on", [P, QT, D], FP32)[:]
    onTh = sb("onTh", [P, DT, TQ], FP16)
    onTl = sb("onTl", [P, DT, TQ], FP16)
    xn2 = sb("xn2", [P, QT, D], FP32)
    stats2 = sb("stats2", [P, QT, 6], FP32)
    mv2 = sb("mv2", [P, QT, 2], FP32)
    rstd2 = sb("rstd2", [P, QT], FP32)
    x2h = sb("x2h", [P, DT, TQ], FP16)
    x2l = sb("x2l", [P, DT, TQ], FP16)
    lg = sb("lg", [P, QT, E], FP32)
    top = sb("top", [P, QT, 8], FP32)
    topi = sb("topi", [P, QT, 8], U32)
    topf = sb("topf", [P, QT, 2], FP32)
    if general:
        mask8 = sb("mask8", [P, QT, TK], U8)
        maskb = sb("maskb", [P, QT, TK], BF16)
    psS = [ctx.enter_context(nc.psum_tensor(f"{path.name}_psS{i}", [P, 512], FP32)) for i in range(2)]
    psT = [ctx.enter_context(nc.psum_tensor(f"{path.name}_psT{i}", [P, 512], FP32)) for i in range(2)]
    psV = [ctx.enter_context(nc.psum_tensor(f"{path.name}_psV{i}", [P, 512], FP32)) for i in range(2)]
    psM = [ctx.enter_context(nc.psum_tensor(f"{path.name}_psM{i}", [P, 512], FP32)) for i in range(2)]
    qstk, kstk = scratch["qstk"], scratch["kstk"]
    x_v = io["x"].rearrange("b (t p) d -> b p t d", p=P)
    c_v = io["ctx"].rearrange("b (c t p) d -> b c p t d", p=P, t=2)
    m_v = io["mask"].rearrange("b (t p) k -> b p t k", p=P)
    UNITS = 2 * C * GROUPS

    def kv(u, c):
        return c if general else u

    def batches(eng, body):
        if general:
            with eng.Fori(0, B) as b:
                body(b, 0)
            return
        with eng.Fori(0, B // 2 - 1) as pair:
            body(pair * 2, 0)
            body(pair * 2 + 1, 1)
        body(B - 2, 0)
        body(B - 1, 1)

    def follows(b, n):
        return not isinstance(b, int) or b + n < B

    nc.disable_value_cache = general
    block = ctx.enter_context(nc.Block())

    @block.sync
    def _(sp):
        def until_sp(name, count):
            until(sp, name, count, alone=True)

        def load_x(b):
            until_sp("xn_ready", of("xn_ready", b, 0))
            sp.dma_start(xbuf[:], x_v[b]).then_inc(sem["x_loaded"], 16)

        def load_ctx(b, i):
            until_sp("cT_mm", of("cT_mm", b, i))
            sp.dma_start(cbuf[:], c_v[b, path.chunks[i]]).then_inc(sem["ctx_loaded"], 16)

        def load_res(b):
            until_sp("acc_done", of("acc_done", b, 0))
            until_sp("xn2_ready", of("xn2_ready", b, 0))
            sp.dma_start(xres[:], x_v[b]).then_inc(sem["res_loaded"], 16)

        def stack_q(b, u):
            until_sp("qs_loaded", of("qs_loaded", b, 0))
            for part, (tile, done) in enumerate(((qh, "qh"), (ql, "ql"))):
                until_sp(done, of(done, b, DT))
                sp.dma_start(qstk[part].rearrange("(o p) q -> p o q", p=P), tile[:]).then_inc(sem["qstk_w"], 16)
            until_sp("qstk_w", of("qstk_w", b, 32))
            until_sp("st_mm", of("st_mm", b - NB + 1, 0))
            for j in range(2):
                for s, part in enumerate((0, 1, 0)):
                    r = 64 * j + DH * s
                    src = qstk[part].rearrange("(t j r) q -> j r t q", j=2, r=DH)
                    sp.dma_start(Qs[u][r:r + DH, :, :], src[j]).then_inc(sem["qs_loaded"], 16)
                r = 64 * j + 48
                sp.dma_start(Qs[u][r:r + 1, :, :], scratch["zero_row"][:, 0:NPAIR, :]).then_inc(sem["qs_loaded"], 16)

        def stack_k(b, u, i):
            n = sem_per["kz_loaded"] // C
            until_sp("kz_loaded", of("kz_loaded", b, n * i))
            for part, (tile, done) in enumerate(((kh, "kh"), (kl, "kl"))):
                until_sp(done, of(done, b, i + 1))
                sp.dma_start(kstk[part].rearrange("(o p) k -> p o k", p=P), tile[:]).then_inc(sem["kstk_w"], 16)
            until_sp("kstk_w", of("kstk_w", b, 32 * (i + 1)))
            until_sp("st_mm", of("st_mm", b - NB + 1, 0))
            for j in range(2):
                for s, part in enumerate((0, 0, 1)):
                    r = 64 * j + DH * s
                    src = kstk[part].rearrange("(t j r) k -> j r t k", j=2, r=DH)
                    sp.dma_start(Kz[kv(u, i)][r:r + DH, :, j, :], src[j]).then_inc(sem["kz_loaded"], 16)
                if not general:
                    r = 64 * j + 49
                    row = scratch["kmask"][bass.ds(b, 1), path.chunks[i] * KC:(path.chunks[i] + 1) * KC]
                    sp.dma_start(Kz[kv(u, i)][r:r + MASK_ROWS, :, j, :],
                                 row.unsqueeze(1).to_broadcast([MASK_ROWS, NPAIR, KC])).then_inc(sem["kz_loaded"], 16)

        def extra_rows():
            until_sp("cleared", 1)
            for j in range(2):
                r = 64 * j + 48
                for tile in Qs:
                    sp.dma_start(tile[r:r + DH, :, :], scratch["q_rows"].unsqueeze(1).to_broadcast([DH, NPAIR, TQ]))\
                        .then_inc(sem["extras"], 16)
                for tile in Kz:
                    sp.dma_start(tile[r:r + DH, :, j, :],
                                 scratch["k_rows"].unsqueeze(1).to_broadcast([DH, NPAIR, KC])).then_inc(sem["extras"], 16)
            until_sp("extras", sem_per["extras"])

        def max_rows(b, u):
            until_sp("mT_ready", of("mT_ready", b, 1))
            until_sp("m_rows", of("m_rows", b, 0))
            sp.dma_start(scratch["max_rows"], mT16[:]).then_inc(sem["m_saved"], 16)
            until_sp("m_saved", of("m_saved", b, 16))
            for j in range(2):
                sp.dma_start(Qs[u][64 * j + 48:64 * j + 49, :, :],
                             scratch["max_rows"].rearrange("(o t j) q -> j o t q", j=2, o=1)[j])\
                    .then_inc(sem["m_rows"], 16)

        def save_xn2(b):
            until_sp("xn2_ready", of("xn2_ready", b, 1))
            sp.dma_start(keep["xn2"][:, bass.ds(b * QT, QT), :], xn2[:]).then_inc(sem["xn2_saved"], 16)

        extra_rows()
        if general:
            with sp.Fori(0, B) as b:
                until_sp("st_mm", of("st_mm", b, 0))
                sp.dma_start(mask8[:], m_v[b]).then_inc(sem["mask_loaded"], 16)
                load_x(b)
                for i in range(C):
                    load_ctx(b, i)
                    if i == 0:
                        load_res(b)
                        stack_q(b, 0)
                    stack_k(b, 0, i)
                max_rows(b, 0)
                save_xn2(b)
            until_sp("xn2_saved", of("xn2_saved", B, 0))
            return
        for b in range(2):
            load_x(b)
            load_ctx(b, 0)
            stack_q(b, b)
            stack_k(b, b, 0)
        max_rows(0, 0)

        def slot(b, u):
            if follows(b, 2):
                load_x(b + 2)
                load_ctx(b + 2, 0)
            load_res(b)
            if follows(b, 1):
                max_rows(b + 1, 1 - u)
            if follows(b, 2):
                stack_q(b + 2, u)
                stack_k(b + 2, u, 0)
            save_xn2(b)
        batches(sp, slot)
        until_sp("xn2_saved", of("xn2_saved", B, 0))

    @block.tensor
    def _(pe):
        held = [None, None]

        def misc(what, b, reader, k=1):
            bank = MISC[what]
            if held[bank]:
                until(pe, *held[bank])
            held[bank] = (reader, of(reader, b, k))
            return psM[bank]

        def transposes(what, b, src, done, reader):
            for dt in range(DT):
                ps = misc(f"{what}{dt}", b, reader, dt + 1)
                for t in range(QT):
                    mm = nc.tensor.transpose(ps[:, t * P:(t + 1) * P], src[:, t, dt * P:(dt + 1) * P], keep["ident"][:])
                mm.then_inc(sem[done], 1)

        def split_product(out, left, right, cols):
            terms = [(left[0], right[0]), (left[0], right[1]), (left[1], right[0])]
            for dt in range(DT):
                for n, (a, w) in enumerate(terms):
                    mm = nc.tensor.matmul(out, a(dt), w(dt), start=(dt == 0 and n == 0),
                                          stop=(dt == DT - 1 and n == 2))
            return mm

        def w_cols(w, part, lo, n):
            return lambda dt: keep[f"{w}{part}"][:, dt, lo:lo + n]

        def xT(b):
            until(pe, "xn_ready", of("xn_ready", b, 1))
            transposes("xT", b, xn, "xT_mm", "xTl")

        def cT(b, i):
            until(pe, "ctx_loaded", of("ctx_loaded", b, 16 * (i + 1)))
            ps = misc("cT", b, "cTl", i + 1)
            for dt in range(DT):
                for t in range(2):
                    mm = nc.tensor.transpose(ps[:, dt * KC + t * P:dt * KC + (t + 1) * P],
                                             cbuf[:, t, dt * P:(dt + 1) * P], keep["ident"][:])
            mm.then_inc(sem["cT_mm"], 1)

        def q_proj(b):
            until(pe, "xTl", of("xTl", b, 2))
            for o in range(DT):
                ps = misc(f"Q{o}", b, "qf", o + 1)
                split_product(ps[:], (w_cols("Wq", "h", o * P, P), w_cols("Wq", "l", o * P, P)),
                              (lambda dt: xTh[:, dt, :], lambda dt: xTl[:, dt, :]), TQ).then_inc(sem["q_mm"], 1)

        def kv_proj(b, i):
            until(pe, "cTl", of("cTl", b, i + 1))
            ps = misc("K", b, "kf", i + 1)
            for o in range(DT):
                mm = split_product(ps[:, o * KC:(o + 1) * KC], (w_cols("Wk", "h", o * P, P), w_cols("Wk", "l", o * P, P)),
                                   (lambda dt: cTh[:, dt, :], lambda dt: cTl[:, dt, :]), KC)
            mm.then_inc(sem["k_mm"], 1)
            ps = misc("V", b, "v_ready", i + 1)
            for t in range(2):
                mm = split_product(ps[:, t * D:(t + 1) * D],
                                   (lambda dt: cTh[:, dt, t * P:(t + 1) * P], lambda dt: cTl[:, dt, t * P:(t + 1) * P]),
                                   (w_cols("Wv", "h", 0, D), w_cols("Wv", "l", 0, D)), D)
            mm.then_inc(sem["v_mm"], 1)

        def scores(b, u, n):
            t, p, c = n // (NPAIR * C), n // C % NPAIR, n % C
            until(pe, "max_done", of("max_done", b, n - 1))
            out = psS[n % 2]
            mm = nc.tensor.matmul(out[:], Qs[u][:, p, t * P:(t + 1) * P], Kz[kv(u, c)][:, p, :, :],
                                  start=True, stop=not general)
            if general:
                for j in range(2):
                    mm = nc.tensor.matmul(out[:, j * KC:(j + 1) * KC], keep["negI"][:],
                                          maskb[:, t, c * KC:(c + 1) * KC], start=False, stop=(j == 1))
            mm.then_inc(sem["s_mm"], 1)

        def stacks_ready(b):
            until(pe, "qs_loaded", of("qs_loaded", b + 1, 0))
            until(pe, "kz_loaded", of("kz_loaded", b + 1, 0))
            if general:
                until(pe, "mask_ready", of("mask_ready", b, 1))

        def mT(b):
            if C == 1:
                until(pe, "max_done", of("max_done", b, 32))
            else:
                until(pe, "negm", of("negm", b, 1))
            ps = misc("mT", b, "mT_ready")
            for t in range(QT):
                mm = nc.tensor.transpose(ps[0:H, t * P:(t + 1) * P], negm[:, t, :], keep["ident"][:])
            mm.then_inc(sem["mT_mm"], 1)

        def scores_T(b, u, n):
            g, kb, i = n // (8 * C), n // 4 % (2 * C), n % 4
            h = 4 * g + i
            if n == 0:
                until(pe, "m_rows", of("m_rows", b, 32))
            until(pe, "exp_done", of("exp_done", b, n - 1))
            out = psT[n % 2]
            mm = nc.tensor.matmul(out[:], Kz[kv(u, kb // 2)][:, h // 2, h % 2, (kb % 2) * P:(kb % 2 + 1) * P],
                                  Qs[u][:, h // 2, :], start=True, stop=not general)
            if general:
                for t in range(QT):
                    mm = nc.tensor.matmul(out[:, t * P:(t + 1) * P], maskb[:, t, kb * P:(kb + 1) * P],
                                          keep["negI"][:], start=False, stop=(t == QT - 1))
            mm.then_inc(sem["st_mm"], 1)

        def weighted(b, u, k):
            g, kb = k // (2 * C), k % (2 * C)
            until(pe, "exp_done", of("exp_done", b, 4 * k + 4))
            if k == 0:
                until(pe, "v_ready", of("v_ready", b, C))
            if kb == 0:
                until(pe, "oT_ready", of("oT_ready", b, g - 1))
            for i in range(4):
                mm = nc.tensor.matmul(psV[g % 2][32 * i:32 * i + 32, :], V[kv(u, kb // 2)][:, kb % 2, 4 * g + i, :],
                                      PT[:, (4 * k + i) % NPT, :], start=(kb == 0), stop=(kb == 2 * C - 1),
                                      skip_group_check=True)
            mm.then_inc(sem["pv_mm"], 1)

        def oX(b, g):
            until(pe, "oT_ready", of("oT_ready", b, g + 1))
            ps = misc(f"oX{g}", b, "on_ready", g + 1)
            for t in range(QT):
                mm = nc.tensor.transpose(ps[:, t * P:(t + 1) * P], oT[:, g % 2, t * P:(t + 1) * P], keep["ident"][:])
            mm.then_inc(sem["oX_mm"], 1)

        def onT(b):
            until(pe, "on_ready", of("on_ready", b, GROUPS))
            transposes("onT", b, on, "onT_mm", "onTl")

        def o_proj(b):
            until(pe, "onTl", of("onTl", b, 2))
            for k in range(2):
                ps = misc(f"O{k}", b, "x1_done", k + 1)
                for j in range(2):
                    lo = (2 * k + j) * P
                    mm = split_product(ps[:, j * D:(j + 1) * D],
                                       (lambda dt: onTh[:, dt, lo:lo + P], lambda dt: onTl[:, dt, lo:lo + P]),
                                       (w_cols("Wo", "h", 0, D), w_cols("Wo", "l", 0, D)), D)
                mm.then_inc(sem["o_mm"], 1)

        def x2T(b):
            until(pe, "xn2_ready", of("xn2_ready", b, 1))
            transposes("x2T", b, xn2, "x2T_mm", "x2l")

        def router(b):
            until(pe, "x2l", of("x2l", b, 2))
            ps = misc("R", b, "rt_link")
            for t in range(QT):
                mm = split_product(ps[:, t * E:(t + 1) * E],
                                   (lambda dt: x2h[:, dt, t * P:(t + 1) * P], lambda dt: x2l[:, dt, t * P:(t + 1) * P]),
                                   (w_cols("Wr", "h", 0, E), w_cols("Wr", "l", 0, E)), E)
            mm.then_inc(sem["r_mm"], 1)

        def last_of(b):
            return [("rt_link", of("rt_link", b, 1)), ("x2l", of("x2l", b, 2))]

        until(pe, "extras", sem_per["extras"])
        if general:
            with pe.Fori(0, B) as b:
                held[:] = last_of(b - 1)
                xT(b)
                for i in range(C):
                    cT(b, i)
                    if i == 0:
                        q_proj(b)
                    kv_proj(b, i)
                stacks_ready(b)
                for n in range(32 * C):
                    scores(b, 0, n)
                mT(b)
                for k in range(UNITS):
                    for i in range(4):
                        scores_T(b, 0, 4 * k + i)
                    weighted(b, 0, k)
                    if k % (2 * C) == 2 * C - 1:
                        oX(b, k // (2 * C))
                onT(b)
                o_proj(b)
                x2T(b)
                router(b)
            return
        for b in range(2):
            xT(b)
            cT(b, 0)
            q_proj(b)
            kv_proj(b, 0)
        stacks_ready(0)
        for n in range(32):
            scores(0, 0, n)
        mT(0)
        for bank in held:
            until(pe, *bank)

        def slot(b, u):
            held[:] = last_of(b - 1)
            for i in range(4):
                scores_T(b, u, i)
            if follows(b, 1):
                stacks_ready(b + 1)
            for k in range(UNITS):
                for i in range(4):
                    if k + 1 < UNITS:
                        scores_T(b, u, 4 * (k + 1) + i)
                    if follows(b, 1):
                        scores(b + 1, 1 - u, 4 * k + i)
                weighted(b, u, k)
                if k in (3, 5, 7):
                    oX(b, (k - 3) // 2)
            if follows(b, 1):
                mT(b + 1)
            oX(b, 3)
            if follows(b, 2):
                xT(b + 2)
            onT(b)
            if follows(b, 2):
                cT(b + 2, 0)
            o_proj(b)
            if follows(b, 2):
                q_proj(b + 2)
                kv_proj(b + 2, 0)
            x2T(b)
            router(b)
        batches(pe, slot)

    @block.scalar
    def _(act):
        def high(what, dst, b, after, done, n=DT):
            for dt in range(n):
                until(act, after, of(after, b, dt + 1))
                nc.scalar.activation(dst[:, dt, :], psM[MISC[f"{what}{dt}"]][:], ACT.Copy).then_inc(sem[done], 1)

        def xT_high(b):
            until(act, "q_mm", of("q_mm", b, 0))
            high("xT", xTh, b, "xT_mm", "xTh")

        def cT_high(b, i):
            until(act, "v_mm", of("v_mm", b, i))
            until(act, "cT_mm", of("cT_mm", b, i + 1))
            nc.scalar.activation(cTh[:].rearrange("p a k -> p (a k)"), psM[MISC["cT"]][:], ACT.Copy).then_inc(sem["cTh"], 1)

        def q_high(b):
            until(act, "qstk_w", of("qstk_w", b, 0))
            for o in range(DT):
                until(act, "qf", of("qf", b, o + 1))
                nc.scalar.activation(qh[:, o, :], qf[:, o, :], ACT.Copy).then_inc(sem["qh"], 1)

        def k_high(b, i):
            until(act, "kstk_w", of("kstk_w", b, 32 * i))
            until(act, "kf", of("kf", b, i + 1))
            nc.scalar.activation(kh[:].rearrange("p a k -> p (a k)"), kf[:].rearrange("p a k -> p (a k)"),
                                 ACT.Copy).then_inc(sem["kh"], 1)

        def max_T(b):
            until(act, "m_rows", of("m_rows", b, 0))
            until(act, "mT_mm", of("mT_mm", b, 1))
            nc.scalar.activation(mT16[:], psM[MISC["mT"]][0:H, :], ACT.Copy).then_inc(sem["mT_ready"], 1)

        def exps(b, k):
            for i in range(4):
                n = 4 * k + i
                until(act, "st_mm", of("st_mm", b, n + 1))
                if i == 0:
                    until(act, "pv_mm", of("pv_mm", b, k + 1 - NPT // 4))
                nc.scalar.activation(PT[:, n % NPT, :], psT[n % 2][:], ACT.Exp).then_inc(sem["exp_done"], 1)

        def out_T(b, g):
            until(act, "oX_mm", of("oX_mm", b, g - 1))
            until(act, "pv_mm", of("pv_mm", b, 2 * C * (g + 1)))
            nc.scalar.activation(oT[:, g % 2, :], psV[g % 2][:], ACT.Copy).then_inc(sem["oT_ready"], 1)

        def onT_high(b):
            until(act, "o_mm", of("o_mm", b, 0))
            high("onT", onTh, b, "onT_mm", "onTh")

        def x2_high(b):
            until(act, "r_mm", of("r_mm", b, 0))
            high("x2T", x2h, b, "x2T_mm", "x2h")

        if general:
            with act.Fori(0, B) as b:
                xT_high(b)
                for i in range(C):
                    cT_high(b, i)
                    if i == 0:
                        q_high(b)
                    k_high(b, i)
                max_T(b)
                for k in range(UNITS):
                    exps(b, k)
                    if k % (2 * C) == 2 * C - 1:
                        out_T(b, k // (2 * C))
                onT_high(b)
                x2_high(b)
            return
        for b in range(2):
            xT_high(b)
            cT_high(b, 0)
            q_high(b)
            k_high(b, 0)
        max_T(0)

        def slot(b, u):
            for k in range(UNITS):
                exps(b, k)
                if k in (2, 4, 6):
                    out_T(b, (k - 2) // 2)
            out_T(b, 3)
            if follows(b, 1):
                max_T(b + 1)
            if follows(b, 2):
                xT_high(b + 2)
            onT_high(b)
            if follows(b, 2):
                cT_high(b + 2, 0)
                q_high(b + 2)
                k_high(b + 2, 0)
            x2_high(b)
        batches(act, slot)

    @block.vector
    def _(dve):
        def low(what, dst, hi, b, after, done):
            for dt in range(DT):
                until(dve, after, of(after, b, dt + 1))
                nc.vector.tensor_tensor(dst[:, dt, :], psM[MISC[f"{what}{dt}"]][:], hi[:, dt, :],
                                        ALU.subtract).then_inc(sem[done], 1)

        def moments(b, src, st, mom, link):
            for t in range(QT):
                ins = nc.vector.bn_stats(st[:, t, :], src[:, t, :])
            ins.then_inc(sem[link], 1)
            until(dve, link, of(link, b, 1), alone=True)
            for t in range(QT):
                ins = nc.vector.bn_aggr(mom[:, t, :], st[:, t, :])
            ins.then_inc(sem[link], 1)

        def normalise(src, mom, rs, dst):
            for t in range(QT):
                ins = nc.vector.tensor_scalar(dst[:, t, :], src[:, t, :], mom[:, t, 0:1], rs[:, t:t + 1],
                                              ALU.subtract, ALU.mult)
            return ins

        def ln1_moments(b):
            until(dve, "x_loaded", of("x_loaded", b, 16), alone=True)
            moments(b, xbuf, stats, mv, "ln1_link")

        def ln1(b):
            until(dve, "rstd1", of("rstd1", b, 1))
            until(dve, "xT_mm", of("xT_mm", b, 0))
            normalise(xbuf, mv, rstd, xn).then_inc(sem["xn_ready"], 1)

        def xT_low(b):
            until(dve, "q_mm", of("q_mm", b, 0))
            low("xT", xTl, xTh, b, "xTh", "xTl")

        def cT_low(b, i):
            until(dve, "cTh", of("cTh", b, i + 1))
            nc.vector.tensor_tensor(cTl[:].rearrange("p a k -> p (a k)"), psM[MISC["cT"]][:],
                                    cTh[:].rearrange("p a k -> p (a k)"), ALU.subtract).then_inc(sem["cTl"], 1)

        def q_bias(b):
            for o in range(DT):
                until(dve, "ql", of("ql", b - 1, o + 1))
                until(dve, "q_mm", of("q_mm", b, o + 1))
                nc.vector.tensor_scalar(qf[:, o, :], psM[MISC[f"Q{o}"]][:], keep["bqk"][:, o:o + 1], DH ** -0.5,
                                        ALU.add, ALU.mult).then_inc(sem["qf"], 1)

        def k_bias(b, u, i):
            until(dve, "kl", of("kl", b, i))
            until(dve, "k_mm", of("k_mm", b, i + 1))
            for o in range(DT):
                ins = nc.vector.tensor_scalar(kf[:, o, :], psM[MISC["K"]][:, o * KC:(o + 1) * KC],
                                              keep["bqk"][:, 2 + o:3 + o], None, ALU.add)
            ins.then_inc(sem["kf"], 1)
            until(dve, "pv_mm", of("pv_mm", b - NB + 1, 0))
            until(dve, "v_mm", of("v_mm", b, i + 1))
            for t in range(2):
                ins = nc.vector.tensor_tensor(V[kv(u, i)][:, t, :, 0:DH],
                                              psM[MISC["V"]][:, t * D:(t + 1) * D].rearrange("p (h r) -> p h r", h=H),
                                              keep["bv"][:].rearrange("p (h r) -> p h r", h=H), ALU.add)
            ins.then_inc(sem["v_ready"], 1)

        def maximum(b, n):
            t, p, c = n // (NPAIR * C), n // C % NPAIR, n % C
            until(dve, "s_mm", of("s_mm", b, n + 1))
            if n == 0:
                until(dve, "mT_mm", of("mT_mm", b, 0))
            src = psS[n % 2][:].rearrange("p (j k) -> p j k", j=2)
            if C == 1:
                nc.vector.tensor_reduce(negm[:, t, 2 * p:2 * p + 2], src, AX.X, ALU.max,
                                        negate=True).then_inc(sem["max_done"], 1)
            else:
                nc.vector.tensor_reduce(mx[:, t, 2 * p:2 * p + 2, c], src, AX.X, ALU.max).then_inc(sem["max_done"], 1)

        def row_max(b):
            if C > 1:
                until(dve, "max_done", of("max_done", b, 32 * C))
                nc.vector.tensor_reduce(negm[:].rearrange("p t h -> p (t h)"), mx[:].rearrange("p t h c -> p (t h) c"),
                                        AX.X, ALU.max, negate=True).then_inc(sem["negm"], 1)

        def normalised_out(b, g):
            k = MISC[f"oX{g}"]
            until(dve, "oX_mm", of("oX_mm", b, g + 1))
            src = psM[k][:].rearrange("p (t i r) -> p t i r", t=QT, i=4)
            until(dve, "on_ready", of("on_ready", b, g))
            nc.vector.reciprocal(rec[:], src[:, :, :, DH]).then_inc(sem["rec"], 1)
            until(dve, "rec", of("rec", b, g + 1))
            if g == 0:
                until(dve, "onT_mm", of("onT_mm", b, 0))
            dst = on.rearrange("p t (h r) -> p t h r", h=H)[:, :, 4 * g:4 * g + 4, :]
            nc.vector.tensor_tensor(dst, src[:, :, :, 0:DH], rec[:].unsqueeze(3).to_broadcast([P, QT, 4, DH]),
                                    ALU.mult).then_inc(sem["on_ready"], 1)

        def onT_low(b):
            until(dve, "o_mm", of("o_mm", b, 0))
            low("onT", onTl, onTh, b, "onTh", "onTl")

        def residual(b):
            until(dve, "res_ready", of("res_ready", b, 1))
            for k in range(2):
                until(dve, "o_mm", of("o_mm", b, k + 1))
                dst = xres[:, 2 * k:2 * k + 2, :].rearrange("p t d -> p (t d)")
                nc.vector.tensor_tensor(dst, psM[MISC[f"O{k}"]][:], dst, ALU.add).then_inc(sem["x1_done"], 1)

        def ln2_moments(b):
            until(dve, "x1_done", of("x1_done", b, 2), alone=True)
            moments(b, xres, stats2, mv2, "ln2_link")

        def ln2(b):
            until(dve, "rstd2", of("rstd2", b, 1))
            until(dve, "x2T_mm", of("x2T_mm", b, 0))
            until(dve, "xn2_saved", of("xn2_saved", b, 0))
            normalise(xres, mv2, rstd2, xn2).then_inc(sem["xn2_ready"], 1)

        def x2_low(b):
            until(dve, "r_mm", of("r_mm", b, 0))
            low("x2T", x2l, x2h, b, "x2h", "x2l")

        def route(b):
            until(dve, "r_mm", of("r_mm", b, 1))
            until(dve, "rt_link", of("rt_link", b, 0))
            nc.vector.tensor_tensor(lg[:], psM[MISC["R"]][:, 0:QT * E].rearrange("p (t e) -> p t e", t=QT),
                                    keep["br"][:].unsqueeze(1).to_broadcast([P, QT, E]), ALU.add).then_inc(sem["rt_link"], 1)
            until(dve, "rt_link", of("rt_link", b, 1), alone=True)
            for t in range(QT):
                ins = nc.vector.max(top[:, t, :], lg[:, t, :])
            ins.then_inc(sem["rt_link"], 1)
            until(dve, "rt_link", of("rt_link", b, 2), alone=True)
            for t in range(QT):
                ins = nc.vector.max_index(topi[:, t, :], top[:, t, :], lg[:, t, :])
            ins.then_inc(sem["rt_link"], 1)
            until(dve, "rt_link", of("rt_link", b, 3))
            nc.vector.tensor_copy(topf[:], topi[:, :, 0:2]).then_inc(sem["rt_link"], 1)
            nc.vector.tensor_tensor(keep["gap"][:, bass.ds(b * QT, QT)], top[:, :, 1], top[:, :, 0], ALU.subtract)
            until(dve, "rt_link", of("rt_link", b, 4))
            for k in range(2):
                ins = nc.vector.tensor_tensor(keep["pick"][:, k, bass.ds(b * QT, QT), :],
                                              keep["iota_e"][:].unsqueeze(1).to_broadcast([P, QT, E]),
                                              topf[:, :, k:k + 1].to_broadcast([P, QT, E]), ALU.is_equal)
            ins.then_inc(sem["rt_link"], 1)

        if general:
            with dve.Fori(0, B) as b:
                until(dve, "mask_loaded", of("mask_loaded", b, 16))
                until(dve, "st_mm", of("st_mm", b, 0))
                nc.vector.tensor_copy(maskb[:], mask8[:]).then_inc(sem["mask_ready"], 1)
                ln1_moments(b)
                ln1(b)
                xT_low(b)
                for i in range(C):
                    cT_low(b, i)
                    if i == 0:
                        q_bias(b)
                    k_bias(b, 0, i)
                for n in range(32 * C):
                    maximum(b, n)
                row_max(b)
                for g in range(GROUPS):
                    normalised_out(b, g)
                onT_low(b)
                residual(b)
                ln2_moments(b)
                ln2(b)
                x2_low(b)
                route(b)
            return
        for b in range(2):
            ln1_moments(b)
            ln1(b)
            xT_low(b)
            cT_low(b, 0)
            q_bias(b)
            k_bias(b, b, 0)
        for n in range(32):
            maximum(0, n)
        row_max(0)

        def slot(b, u):
            for k in range(UNITS):
                if follows(b, 1):
                    for i in range(4):
                        maximum(b + 1, 4 * k + i)
                if k in (3, 5, 7):
                    normalised_out(b, (k - 3) // 2)
                if k == 4 and follows(b, 2):
                    ln1_moments(b + 2)
                if k == 6 and follows(b, 2):
                    ln1(b + 2)
            if follows(b, 1):
                row_max(b + 1)
            normalised_out(b, 3)
            if follows(b, 2):
                xT_low(b + 2)
            onT_low(b)
            if follows(b, 2):
                cT_low(b + 2, 0)
            residual(b)
            ln2_moments(b)
            if follows(b, 2):
                q_bias(b + 2)
            ln2(b)
            if follows(b, 2):
                k_bias(b + 2, u, 0)
            x2_low(b)
            route(b)
        batches(dve, slot)

    @block.gpsimd
    def _(pool):
        def rstd_of(b, mom, link, rs, done, half):
            until(pool, link, of(link, b, 2))
            until(pool, done, of(done, b, 0), alone=True)
            nc.gpsimd.tensor_scalar(rs[:], mom[:, :, 1], EPS, None, ALU.add).then_inc(sem[half], 1)
            until(pool, half, of(half, b, 1))
            nc.gpsimd.tensor_tensor(rs[:], rs[:], keep["minus_half"][:], ALU.pow).then_inc(sem[done], 1)

        def q_low(b):
            until(pool, "qstk_w", of("qstk_w", b, 0))
            for o in range(DT):
                until(pool, "qh", of("qh", b, o + 1))
                nc.gpsimd.tensor_tensor(ql[:, o, :], qf[:, o, :], qh[:, o, :], ALU.subtract).then_inc(sem["ql"], 1)

        def k_low(b, i):
            until(pool, "kstk_w", of("kstk_w", b, 32 * i))
            until(pool, "kh", of("kh", b, i + 1))
            nc.gpsimd.tensor_tensor(kl[:].rearrange("p a k -> p (a k)"), kf[:].rearrange("p a k -> p (a k)"),
                                    kh[:].rearrange("p a k -> p (a k)"), ALU.subtract).then_inc(sem["kl"], 1)

        def res_bias(b):
            until(pool, "res_loaded", of("res_loaded", b, 16))
            for t in range(QT):
                ins = nc.gpsimd.tensor_tensor(xres[:, t, :], xres[:, t, :], keep["bo"][:], ALU.add)
            ins.then_inc(sem["res_ready"], 1)

        def keep_x1(b):
            until(pool, "x1_done", of("x1_done", b, 2))
            for t in range(QT):
                ins = nc.gpsimd.tensor_tensor(keep["acc"][:, bass.ds(b * QT + t, 1), :].rearrange("p o d -> p (o d)"),
                                              xres[:, t, :], keep["bs2"][:], ALU.add)
            ins.then_inc(sem["acc_done"], 1)

        def rstd1(b):
            rstd_of(b, mv, "ln1_link", rstd, "rstd1", "ve1")

        def rstd2_(b):
            rstd_of(b, mv2, "ln2_link", rstd2, "rstd2", "ve2")

        for tile in Kz:
            nc.gpsimd.memset(tile[:], 0.0)
        for tile in V:
            nc.gpsimd.memset(tile[:, :, :, DH + 1:32], 0.0)
            ins = nc.gpsimd.memset(tile[:, :, :, DH:DH + 1], 1.0)
        ins.then_inc(sem["cleared"], 1)
        if general:
            with pool.Fori(0, B) as b:
                rstd1(b)
                q_low(b)
                for i in range(C):
                    k_low(b, i)
                res_bias(b)
                rstd2_(b)
                keep_x1(b)
            return
        for b in range(2):
            rstd1(b)
            q_low(b)
            k_low(b, 0)

        def slot(b, u):
            if follows(b, 2):
                rstd1(b + 2)
            res_bias(b)
            rstd2_(b)
            if follows(b, 2):
                q_low(b + 2)
                k_low(b + 2, 0)
            keep_x1(b)
        batches(pool, slot)

    nc.disable_value_cache = False
    ctx.close()


def setup(nc, ctx, io, keep, scratch, path_list):
    inner = ExitStack()

    def sb(name, shape, dt):
        return inner.enter_context(nc.sbuf_tensor(f"setup_{name}", shape, dt))

    def sem(name):
        return ctx.enter_context(nc.semaphore(f"setup_{name}"))

    names = ["Wq", "Wk", "Wv", "Wo"]
    raw = [sb(f"raw{w}", [P, DT, D], FP32) for w in names]
    raw_r = sb("rawWr", [P, DT, E], FP32)
    raw_b = sb("raw_b", [4, P], FP32)
    mask_row = sb("mask_row", [B, TK], U8)
    kmask = sb("kmask", [B, TK], FP16)
    zeros = sb("zeros", [P, 4 * D], FP32)
    WORDS, LASTW = TK // 4, KC // 4
    mask8 = sb("mask8", [P, B, QT, WORDS], I32)
    sums = sb("sums", [P, B, WORDS], I32)
    first = sb("first", [P, B, LASTW], I32)
    first4 = sb("first4", [P, B, LASTW], I32)
    diff = sb("diff", [P, B, WORDS], I32)
    worst = sb("worst", [P, 1], FP32)
    worst_f = sb("worst_f", [P, 1], FP32)
    psO = inner.enter_context(nc.psum_tensor("setup_psO", [1, 1], FP32))
    mask_loaded, summed, odd_link, odd_mm = sem("mask_loaded"), sem("summed"), sem("odd_link"), sem("odd_mm")
    filled, zeroed = sem("filled"), sem("zeroed")
    rows = sb("rows", [DH, 1024], FP16)
    psA = [inner.enter_context(nc.psum_tensor(f"setup_ps{i}", [P, 512], FP32)) for i in range(2)]
    loaded, consts, w_mm, w_high, w_low = sem("loaded"), sem("consts"), sem("w_mm"), sem("w_high"), sem("w_low")
    link, stored, dve_link = sem("link"), sem("stored"), sem("dve_link")
    small = sem("small")
    block = inner.enter_context(nc.Block())

    @block.sync
    def _(sp):
        for i, w in enumerate(names):
            sp.dma_start(raw[i][:], io[w].rearrange("(o p) d -> p o d", p=P)).then_inc(loaded, 16)
        sp.dma_start(raw_r[:], io["Wr"].rearrange("(t p) e -> p t e", p=P)).then_inc(small, 16)
        sp.dma_start(mask_row[:], io["mask"][:, 0, :]).then_inc(small, 16)
        for i, v in enumerate(("bq", "bk")):
            sp.dma_start(raw_b[2 * i:2 * i + 2, :], io[v].rearrange("(o p) -> o p", p=P)).then_inc(small, 16)
        for v in ("bv", "bo", "bs2", "br"):
            sp.dma_start(keep[v][:], io[v].partition_broadcast(P)).then_inc(small, 16)
        sp.dma_start(mask8[:].bitcast(U8), io["mask"].rearrange("b (t p) k -> p b t k", p=P)).then_inc(mask_loaded, 16)
        for b in range(B):
            sp.dma_start(first[:, b, :].bitcast(U8), io["mask"][b, 0, TK - KC:TK].partition_broadcast(P)).then_inc(mask_loaded, 16)
        sp.wait_ge(dve_link, 1)
        sp.dma_start(scratch["kmask"], kmask[:]).then_inc(stored, 16)
        sp.wait_ge(consts, 1)
        sp.dma_start(scratch["q_rows"], rows[:, 0:512]).then_inc(stored, 16)
        sp.dma_start(scratch["k_rows"], rows[:, 512:512 + KC]).then_inc(stored, 16)
        sp.dma_start(scratch["zero_row"], rows[1:2, 512:1024].unsqueeze(1).to_broadcast([1, NPAIR, TQ]))\
            .then_inc(stored, 16)
        for path in path_list:
            path.start_ahead(sp)
        sp.wait_ge(filled, 1)
        with sp.Fori(0, ROWS // (4 * P)) as i:
            sp.dma_start(scratch["xs"][bass.ds(i * 4 * P, 4 * P), :].rearrange("(p r) d -> p (r d)", p=P), zeros[:])\
                .then_inc(zeroed, 16)
        for r in range(2 * N, ROWS, 4 * P):
            sp.dma_start(scratch["ys"][r:r + 4 * P, :].rearrange("(p r) d -> p (r d)", p=P), zeros[:]).then_inc(zeroed, 16)
        sp.wait_ge(small, 16 * 8)
        sp.wait_ge(stored, 64)
        sp.wait_ge(zeroed, 16 * (ROWS + ROWS - 2 * N) // (4 * P))

    @block.gpsimd
    def _(pool):
        nc.gpsimd.memset(rows[:, 0:512], 1.0)
        nc.gpsimd.memset(rows[:, 512:1024], 0.0).then_inc(link, 1)
        pool.wait_ge(link, 1)
        nc.gpsimd.memset(rows[0:1, 0:512], 0.0)
        nc.gpsimd.memset(rows[0:1, 512:512 + KC], 1.0).then_inc(consts, 1)
        nc.gpsimd.memset(keep["minus_half"][:], -0.5)
        nc.gpsimd.memset(zeros[:], 0.0).then_inc(filled, 1)
        nc.gpsimd.memset(keep["ones16"][:], 1.0)
        nc.gpsimd.memset(keep["ones32"][:], 1.0)
        nc.gpsimd.memset(keep["ident"][:], 0.0).then_inc(link, 1)
        nc.gpsimd.iota(keep["iota_i"][:], pattern=[[1, E]], base=0, channel_multiplier=0).then_inc(link, 1)
        pool.wait_ge(link, 3)
        nc.gpsimd.affine_select(out=keep["ident"][:], in_=keep["ident"][:], compare_op=ALU.not_equal, fill=1.0,
                                base=0, pattern=[[-1, P]], channel_multiplier=1).then_inc(consts, 1)
        nc.gpsimd.affine_select(out=keep["below"][:], in_=keep["ones16"][:], compare_op=ALU.is_gt, fill=0.0,
                                base=0, pattern=[[1, P]], channel_multiplier=-1)
        nc.gpsimd.tensor_copy(keep["iota_e"][:], keep["iota_i"][:])
        pool.wait_ge(mask_loaded, 16 * (B + 1))
        for b in range(B):
            nc.gpsimd.tensor_tensor(sums[:, b, :], mask8[:, b, 0, :], mask8[:, b, 1, :], ALU.add).then_inc(summed, 1)
            for t in range(2, QT):
                pool.wait_ge(summed, (QT - 1) * b + t - 1)
                nc.gpsimd.tensor_tensor(sums[:, b, :], sums[:, b, :], mask8[:, b, t, :], ALU.add).then_inc(summed, 1)
        pool.wait_ge(consts, 2)
        nc.gpsimd.tensor_scalar(keep["negI"][:], keep["ident"][:], NEG, None, ALU.mult)

    @block.tensor
    def _(pe):
        pe.wait_ge(consts, 2)
        pe.wait_ge(loaded, 16 * 4)
        for i in range(4):
            if i >= 2:
                pe.wait_ge(w_low, i - 1)
            for dt in range(DT):
                for o in range(DT):
                    mm = nc.tensor.transpose(psA[i % 2][:, dt * D + o * P:dt * D + (o + 1) * P],
                                             raw[i][:, o, dt * P:(dt + 1) * P], keep["ident"][:])
            mm.then_inc(w_mm, 1)
        pe.wait_ge(small, 16 * 8)
        pe.wait_ge(w_low, 3)
        nc.tensor.transpose(psA[0][:, 0:4], raw_b[:], keep["ident"][0:4, 0:4]).then_inc(w_mm, 1)
        pe.wait_ge(odd_link, 4)
        nc.tensor.matmul(psO[:], worst_f[:], keep["ones32"][:], start=True, stop=True).then_inc(odd_mm, 1)

    @block.scalar
    def _(act):
        for i, w in enumerate(names):
            act.wait_ge(w_mm, i + 1)
            nc.scalar.activation(keep[f"{w}h"][:].rearrange("p a d -> p (a d)"), psA[i % 2][:], ACT.Copy).then_inc(w_high, 1)
        act.wait_ge(w_mm, 5)
        nc.scalar.activation(keep["bqk"][:], psA[0][:, 0:4], ACT.Copy)
        act.wait_ge(small, 16 * 8)
        nc.scalar.activation(keep["Wrh"][:], raw_r[:], ACT.Copy).then_inc(w_high, 1)

    @block.vector
    def _(dve):
        dve.wait_ge(small, 16 * 8)
        nc.vector.tensor_scalar(kmask[:], mask_row[:], MASKED, None, ALU.mult).then_inc(dve_link, 1)
        for i, w in enumerate(names):
            dve.wait_ge(w_high, i + 1)
            nc.vector.tensor_tensor(keep[f"{w}l"][:].rearrange("p a d -> p (a d)"), psA[i % 2][:],
                                    keep[f"{w}h"][:].rearrange("p a d -> p (a d)"), ALU.subtract).then_inc(w_low, 1)
        dve.wait_ge(w_high, 5)
        nc.vector.tensor_tensor(keep["Wrl"][:], raw_r[:], keep["Wrh"][:], ALU.subtract)
        steps = [0]

        def then(ins):
            steps[0] += 1
            ins.then_inc(odd_link, 1)
            dve.wait_ge(odd_link, steps[0])

        dve.wait_ge(mask_loaded, 16 * (B + 1))
        then(nc.vector.tensor_scalar(first4[:], first[:], 2, None, ALU.logical_shift_left))
        dve.wait_ge(summed, (QT - 1) * B)
        nc.vector.tensor_scalar(diff[:, :, 0:WORDS - LASTW], sums[:, :, 0:WORDS - LASTW], QT * 0x01010101, None,
                                ALU.bitwise_xor)
        then(nc.vector.tensor_tensor(diff[:, :, WORDS - LASTW:], sums[:, :, WORDS - LASTW:], first4[:], ALU.bitwise_xor))
        then(nc.vector.tensor_reduce(worst[:], diff[:].rearrange("p b w -> p (b w)"), AX.X, ALU.max))
        then(nc.vector.tensor_scalar(worst_f[:], worst[:], 0.0, None, ALU.not_equal))
        dve.wait_ge(odd_mm, 1)
        nc.vector.tensor_copy(keep["odd_i"][:], psO[:])

    inner.close()


def keep_tensors(nc, ctx):
    def sb(name, shape, dt):
        return ctx.enter_context(nc.sbuf_tensor(name, shape, dt))
    keep = {}
    for w, n in (("Wq", D), ("Wk", D), ("Wv", D), ("Wo", D), ("Wr", E)):
        for part in "hl":
            keep[w + part] = sb(w + part, [P, DT, n], FP16)
    keep["bqk"] = sb("bqk", [P, 4], FP32)
    for v, n in (("bv", D), ("bo", D), ("bs2", D), ("br", E)):
        keep[v] = sb(v, [P, n], FP32)
    keep["ident"] = sb("ident", [P, P], FP32)
    keep["negI"] = sb("negI", [P, P], BF16)
    keep["ones16"] = sb("ones16", [P, P], FP16)
    keep["ones32"] = sb("ones32", [P, 1], FP32)
    keep["below"] = sb("below", [P, P], FP16)
    keep["iota_i"] = sb("iota_i", [P, E], I32)
    keep["iota_e"] = sb("iota_e", [P, E], FP32)
    keep["minus_half"] = sb("minus_half", [P, QT], FP32)
    keep["acc"] = sb("acc", [P, NT, D], FP32)
    keep["xn2"] = sb("xn2", [P, NT, D], FP32)
    keep["gap"] = sb("gap", [P, NT], FP32)
    keep["odd_i"] = sb("odd_i", [1, 1], I32)
    keep["pick"] = sb("pick", [P, 2, NT, E], FP16)
    return keep


def scratch_tensors(nc):
    def dram(name, shape, dt):
        return nc.dram_tensor(name, shape, dt).ap()
    return dict(qstk=dram("qstk", [2, D, TQ], FP16), kstk=dram("kstk", [2, D, KC], FP16),
                xs=dram("expert_in", [ROWS, D], FP32), ys=dram("expert_out", [ROWS, D], FP32),
                max_rows=dram("max_rows", [H, TQ], FP16), kmask=dram("kmask_rows", [B, TK], FP16), q_rows=dram("q_rows", [DH, TQ], FP16),
                k_rows=dram("k_rows", [DH, KC], FP16), zero_row=dram("zero_row", [1, NPAIR, TQ], FP16))


NB = 256
NBT = NB // P
NBLK = (2 * N + E * (NB - 1)) // NB
ROWS = (NBLK + 1) * NB
FEW = 4
SH_PAIRS, EX_PAIRS = HS // P, HR // P


class Stage:

    def __init__(self, nc, ctx, name, pairs):
        self.pairs = pairs
        self.per = dict(x_loaded=16, xT_mm=1, xh=1, xl=1, h_mm=pairs, gelu=pairs, act=pairs, acth=pairs,
                        actl=pairs, y_mm=1, y_ready=1, y_stored=16)
        self.ahead = dict(self.per)
        self.passed = ctx.enter_context(nc.semaphore(f"{name}_passed"))
        self.sem = {n: ctx.enter_context(nc.semaphore(f"{name}_{n}")) for n in self.per}

    start_ahead, until, of = Path.start_ahead, Path.until, Path.of


def feed_forward(nc, io, keep, scratch, shared, expert):
    ctx = ExitStack()

    def sb(name, shape, dt):
        return ctx.enter_context(nc.sbuf_tensor(f"ff_{name}", shape, dt))

    def semaphore(name):
        return ctx.enter_context(nc.semaphore(f"ff_{name}"))

    picks = sb("picks", [P, NT, E], FP16)
    PAD = NT // 2
    run = [sb(f"run{i}", [P, PAD + NT, E], FP32) for i in range(2)]
    counts = sb("counts", [P, E], I32)
    blocks_i = sb("blocks_i", [P, E], I32)
    blocks = sb("blocks", [P, E], FP32)
    ones_e = sb("ones_e", [P, E], FP32)
    cum = sb("cum", [P, E], FP32)
    first = sb("first", [P, E], FP32)
    first_i = sb("first_i", [P, E + 1], I32)
    place = sb("place", [P, NT, E], FP32)
    picked = sb("picked", [P, NT, E], FP32)
    posf = sb("posf", [P, 2, NT], FP32)
    pos = sb("pos", [P, 2, NT], I32)
    ratio = sb("ratio", [P, NT], FP32)
    denom = sb("denom", [P, NT], FP32)
    w = [sb(f"w{k}", [P, NT], FP32) for k in range(2)]
    b_raw = sb("b_raw", [P, 3, P], FP32)
    b1T = sb("b1T", [P, 2 * EX_PAIRS * E], FP32)
    bs1T = sb("bs1T", [P, 2 * SH_PAIRS], FP32)
    st1 = sb("st1", [P, DT, 2 * HR], FP32)
    st2 = sb("st2", [P, EX_PAIRS, D], FP32)
    s1 = [sb(f"s1{x}", [P, DT, 2 * HS], FP16) for x in "hl"]
    s2 = [sb(f"s2{x}", [P, SH_PAIRS, D], FP16) for x in "hl"]
    w1 = [[sb(f"w1{x}{u}", [P, DT, 2 * HR], FP16) for x in "hl"] for u in range(2)]
    w2 = [[sb(f"w2{x}{u}", [P, EX_PAIRS, D], FP16) for x in "hl"] for u in range(2)]
    b1 = [sb(f"b1{u}", [P, 2 * EX_PAIRS], FP32) for u in range(2)]
    b2 = [sb(f"b2{u}", [P, D], FP32) for u in range(2)]
    xrow = sb("xrow", [P, NBT, D], FP32)
    xh = sb("xh", [P, DT, NB], FP16)
    xl = sb("xl", [P, DT, NB], FP16)
    gel = sb("gel", [P, 2, NB], FP32)
    actf = sb("actf", [P, 2, NB], FP32)
    acth = sb("acth", [P, EX_PAIRS, NB], FP16)
    actl = sb("actl", [P, EX_PAIRS, NB], FP16)
    ysb = sb("ysb", [P, NBT, D], FP32)
    RING = 6
    yg = sb("yg", [P, RING, 2, D], FP32)

    def bank(name):
        return ctx.enter_context(nc.psum_tensor(f"ff_{name}", [P, 512], FP32))

    psH = [bank(f"psH{i}") for i in range(2)]
    psY = [bank(f"psY{i}") for i in range(2)]
    psX = bank("psX")
    psB, psR, psC = bank("psB"), bank("psR"), bank("psC")

    b_loaded, b_mm, b_ready = semaphore("b_loaded"), semaphore("b_mm"), semaphore("b_ready")
    link, picks_ready, rank_mm = semaphore("link"), semaphore("picks_ready"), semaphore("rank_mm")
    table_ready, pos_ready, ratio_ready = semaphore("table_ready"), semaphore("pos_ready"), semaphore("ratio_ready")
    s_loaded, s_split, s_free = semaphore("s_loaded"), semaphore("s_split"), semaphore("s_free")
    scattered = semaphore("scattered")
    w1_loaded, w2_loaded, b2_loaded = semaphore("w1_loaded"), semaphore("w2_loaded"), semaphore("b2_loaded")
    w_split = semaphore("w_split")
    alone = semaphore("alone")
    gathered = [semaphore(f"gathered{i}") for i in range(RING)]
    mixed, mix_link, stored = semaphore("mixed"), semaphore("mix_link"), semaphore("stored")
    xs, ys = scratch["xs"], scratch["ys"]
    out_v = io["out"].rearrange("b (t p) d -> p (b t) d", p=P)

    def of(stage, name, m, k=0):
        return stage.of(name, m, k)

    def table(eng, which, e, most):
        return eng.value_load(which[0:1, bass.ds(e, 1)], min_val=0, max_val=most)

    def experts(eng, before, body):
        eng.wait_ge(table_ready, 1)
        with eng.Fori(0, E // 2) as half:
            for u in range(2):
                e = half * 2 + u
                n = table(eng, blocks_i, e, N // NB)
                at = table(eng, first_i, e, NBLK - 1)
                if before:
                    before(e, u)

                def own(t):
                    with eng.If(t < n):
                        body(u, nc.s_assert_within(at + t, 0, NBLK - 1, skip_runtime_bounds_check_because=
                                                   "t < n, and an expert's last block is within all experts' blocks"))
                with eng.Fori(0, FEW) as t:
                    own(t)
                with eng.If(n > FEW):
                    with eng.Fori(FEW, N // NB) as t:
                        own(t)

    def shared_blocks(eng, body):
        with eng.Fori(0, N // NB - 1) as m:
            body(m, True)
        body(N // NB - 1, False)

    block = ctx.enter_context(nc.Block())

    @block.sync
    def _(sp):
        sp.dma_start(b_raw[0:72, 0, :], io["be1"].rearrange("e (t p) -> (e t) p", p=P)[0:72, :]).then_inc(b_loaded, 16)
        sp.dma_start(b_raw[0:72, 1, :], io["be1"].rearrange("e (t p) -> (e t) p", p=P)[72:144, :]).then_inc(b_loaded, 16)
        sp.dma_start(b_raw[0:2 * SH_PAIRS, 2, :], io["bs1"].rearrange("(t p) -> t p", p=P)).then_inc(b_loaded, 16)
        sp.dma_start(st1[:, :, 0:2 * HS], io["Ws1"].rearrange("(t p) f -> p t f", p=P)).then_inc(s_loaded, 16)
        sp.dma_start(st2[:, 0:SH_PAIRS, :], io["Ws2"].rearrange("(t p) d -> p t d", p=P)).then_inc(s_loaded, 16)

        def until(stage, name, count):
            stage.until(sp, name, count, alone=True)

        def load_shared(m):
            until(shared, "xT_mm", of(shared, "xT_mm", m))
            sp.dma_start(xrow[:], keep["xn2"][:, bass.ds(m * NBT, NBT), :]).then_inc(shared.sem["x_loaded"], 16)

        load_shared(0)
        with sp.Fori(0, N // NB - 1) as m:
            load_shared(m + 1)
        until(shared, "xT_mm", N // NB)
        sp.wait_ge(scattered, 2 * NT * 16)

        def load_rows(n):
            until(expert, "xT_mm", of(expert, "xT_mm", n))
            rows = xs[bass.ds(n * NB, NB), :].rearrange("(j p) d -> p j d", p=P)
            sp.dma_start(xrow[:], rows).then_inc(expert.sem["x_loaded"], 16)

        load_rows(0)

        def rows_of(u, n):
            load_rows(n + 1)
            until(expert, "y_stored", of(expert, "y_stored", n))
            until(expert, "y_ready", of(expert, "y_ready", n, 1))
            rows = ys[bass.ds(n * NB, NB), :].rearrange("(j p) d -> p j d", p=P)
            sp.dma_start(rows, ysb[:]).then_inc(expert.sem["y_stored"], 16)

        experts(sp, None, rows_of)
        for t in range(0, NT, QT):
            sp.wait_ge(mixed, t + QT)
            sp.dma_start(out_v[:, t:t + QT, :], keep["acc"][:, t:t + QT, :]).then_inc(stored, 16)
        sp.wait_ge(stored, 16 * NT // QT)

    @block.gpsimd
    def _(pool):
        def wait_alone(sem, count):
            pool.wait_ge(sem, count)
            if not isinstance(count, int):
                pool.sem_inc(alone, 1)

        def halves(src, hi, lo, sem, n):
            nc.gpsimd.tensor_scalar(hi, src, 1.0, 0.0, ALU.mult, ALU.add).then_inc(sem, 1)
            pool.wait_ge(sem, n)
            nc.gpsimd.tensor_tensor(lo, src, hi, ALU.subtract).then_inc(sem, 1)

        nc.gpsimd.memset(ones_e[:], 1.0)
        for r in run:
            last = nc.gpsimd.memset(r[:, 0:PAD, :], 0.0)
        last.then_inc(s_free, 1)
        pool.wait_ge(s_loaded, 32)
        n = 0
        for dt in range(DT):
            halves(st1[:, dt, 0:2 * HS], s1[0][:, dt, :], s1[1][:, dt, :], s_split, 2 * n + 1)
            n += 1
        halves(st2[:, 0:SH_PAIRS, :].rearrange("p t d -> p (t d)"), s2[0][:].rearrange("p t d -> p (t d)"),
               s2[1][:].rearrange("p t d -> p (t d)"), s_split, 2 * n + 1)

        def load_w1(e):
            pool.dma_start(st1[:], io["We1"][e].rearrange("(t p) f -> p t f", p=P)).then_inc(w1_loaded, 16)

        def load_w2(e, u):
            pool.dma_start(st2[:], io["We2"][e].rearrange("(t p) d -> p t d", p=P)).then_inc(w2_loaded, 16)

        PER = 2 * DT + 2

        def prepare(e, u, after):
            pool.dma_start(b2[u][:], io["be2"][e].partition_broadcast(P)).then_inc(b2_loaded, 16)
            wait_alone(w1_loaded, e * 16 + 16)
            for dt in range(DT):
                k = 2 * dt
                nc.gpsimd.tensor_scalar(w1[u][0][:, dt, :], st1[:, dt, :], 1.0, 0.0, ALU.mult, ALU.add).then_inc(w_split, 1)
                wait_alone(w_split, e * PER + k + 1)
                nc.gpsimd.tensor_tensor(w1[u][1][:, dt, :], st1[:, dt, :], w1[u][0][:, dt, :], ALU.subtract)\
                    .then_inc(w_split, 1)
            nc.gpsimd.tensor_copy(b1[u][:], b1T[:, bass.ds(e * 2 * EX_PAIRS, 2 * EX_PAIRS)])
            if after:
                wait_alone(w_split, e * PER + 2 * DT)
                load_w1(e + 1)
            wait_alone(w2_loaded, e * 16 + 16)
            flat = [x[:].rearrange("p t d -> p (t d)") for x in (st2, w2[u][0], w2[u][1])]
            nc.gpsimd.tensor_scalar(flat[1], flat[0], 1.0, 0.0, ALU.mult, ALU.add).then_inc(w_split, 1)
            wait_alone(w_split, e * PER + 2 * DT + 1)
            wait_alone(b2_loaded, e * 16 + 16)
            nc.gpsimd.tensor_tensor(flat[2], flat[0], flat[1], ALU.subtract).then_inc(w_split, 1)
            if after:
                wait_alone(w_split, (e + 1) * PER)
                load_w2(e + 1, u)

        pool.wait_ge(s_split, 6)
        load_w1(0)
        load_w2(0, 0)
        pool.wait_ge(pos_ready, 1)
        for t in range(NT):
            for k in range(2):
                pool.indirect_dma_start(out=xs[:, :], out_offset=bass.IndirectOffsetOnAxis(ap=pos[:, k, t:t + 1], axis=0),
                                        in_=keep["xn2"][:, t, :], in_offset=None, bounds_check=ROWS - 1)\
                    .then_inc(scattered, 16)
        pool.wait_ge(b_ready, 3)
        prepare(0, 0, True)
        prepare(1, 1, True)
        pool.wait_ge(table_ready, 1)

        def used(e):
            done = table(pool, first_i, e - 1, NBLK)
            expert.until(pool, "y_ready", done, alone=True)

        with pool.Fori(1, E // 2 - 1) as half:
            for u in range(2):
                used(half * 2 + u)
                prepare(half * 2 + u, u, True)
        for u in range(2):
            used(E - 2 + u)
            prepare(E - 2 + u, u, u == 0)
        total = table(pool, first_i, E, NBLK)
        expert.until(pool, "y_stored", total * 16, alone=True)
        for t in range(NT):
            if t >= RING:
                pool.wait_ge(mixed, t - RING + 1)
            for k in range(2):
                pool.indirect_dma_start(out=yg[:, t % RING, k, :], out_offset=None, in_=ys[:, :],
                                        in_offset=bass.IndirectOffsetOnAxis(ap=pos[:, k, t:t + 1], axis=0),
                                        bounds_check=ROWS - 1).then_inc(gathered[t % RING], 16)

    @block.tensor
    def _(pe):
        pe.wait_ge(b_loaded, 48)
        for i, n in enumerate((72, 72, 2 * SH_PAIRS)):
            mm = nc.tensor.transpose(psB[:, 72 * i:72 * i + n], b_raw[0:n, i, :], keep["ident"][0:n, 0:n])
        mm.then_inc(b_mm, 1)
        pe.wait_ge(picks_ready, 1)
        flat = picks[:].rearrange("p t e -> p (t e)")
        nc.tensor.matmul(psR[:, 0:NT * E], keep["below"][:], flat, start=True, stop=True)
        nc.tensor.matmul(psC[:, 0:NT * E], keep["ones16"][:], flat, start=True, stop=True).then_inc(rank_mm, 1)

        def row_transposes(stage, m):
            stage.until(pe, "x_loaded", of(stage, "x_loaded", m, 16))
            stage.until(pe, "xl", of(stage, "xl", m))
            for dt in range(DT):
                for j in range(NBT):
                    mm = nc.tensor.transpose(psX[:, dt * NB + j * P:dt * NB + (j + 1) * P],
                                             xrow[:, j, dt * P:(dt + 1) * P], keep["ident"][:])
            mm.then_inc(stage.sem["xT_mm"], 1)

        def ffn(stage, m, wa, wb, more):
            n = stage.pairs
            stage.until(pe, "xl", of(stage, "xl", m, 1))
            for j in range(n):
                stage.until(pe, "act", of(stage, "act", m, j - 1))
                for half in range(2):
                    lo = (half * n + j) * P
                    terms = [(wa[0], xh), (wa[0], xl), (wa[1], xh)]
                    for dt in range(DT):
                        for i, (a, x) in enumerate(terms):
                            mm = nc.tensor.matmul(psH[j % 2][:, half * NB:(half + 1) * NB], a[:, dt, lo:lo + P],
                                                  x[:, dt, :], start=(dt == 0 and i == 0), stop=(dt == DT - 1 and i == 2))
                mm.then_inc(stage.sem["h_mm"], 1)
            if more:
                row_transposes(stage, m + 1)
            stage.until(pe, "y_ready", of(stage, "y_ready", m))
            for j in range(n):
                stage.until(pe, "actl", of(stage, "actl", m, j + 1))
                for i in range(NBT):
                    terms = [(acth, wb[0]), (acth, wb[1]), (actl, wb[0])]
                    for s, (a, x) in enumerate(terms):
                        mm = nc.tensor.matmul(psY[i][:, 0:D], a[:, j, i * P:(i + 1) * P], x[:, j, :],
                                              start=(j == 0 and s == 0), stop=(j == n - 1 and s == 2))
            mm.then_inc(stage.sem["y_mm"], 1)

        row_transposes(shared, 0)
        pe.wait_ge(s_split, 6)
        shared_blocks(pe, lambda m, more: ffn(shared, m, s1, s2, more))
        row_transposes(expert, 0)

        def weights_ready(e, u):
            pe.wait_ge(w_split, (e + 1) * (2 * DT + 2))
            pe.sem_inc(alone, 1)

        experts(pe, weights_ready, lambda u, n: ffn(expert, n, w1[u], w2[u], True))

    @block.scalar
    def _(act):
        act.wait_ge(b_mm, 1)
        nc.scalar.activation(b1T[:], psB[:, 0:144], ACT.Copy).then_inc(b_ready, 1)
        nc.scalar.activation(bs1T[:], psB[:, 144:144 + 2 * SH_PAIRS], ACT.Copy).then_inc(b_ready, 1)
        nc.scalar.activation(ratio[:], keep["gap"][:], ACT.Exp, scale=1.0 / TAU).then_inc(ratio_ready, 1)
        act.wait_ge(b_ready, 2)
        act.sem_inc(b_ready, 1)

        def row_high(stage, m):
            stage.until(act, "xT_mm", of(stage, "xT_mm", m, 1))
            nc.scalar.activation(xh[:].rearrange("p t n -> p (t n)"), psX[:], ACT.Copy).then_inc(stage.sem["xh"], 1)

        def ffn(stage, m, bias, more):
            n = stage.pairs

            def high(j):
                stage.until(act, "act", of(stage, "act", m, j + 1))
                if j == 0:
                    stage.until(act, "y_mm", of(stage, "y_mm", m))
                nc.scalar.activation(acth[:, j, :], actf[:, j % 2, :], ACT.Copy).then_inc(stage.sem["acth"], 1)

            for j in range(n):
                stage.until(act, "act", of(stage, "act", m, j - 1))
                stage.until(act, "h_mm", of(stage, "h_mm", m, j + 1))
                nc.scalar.activation(gel[:, j % 2, :], psH[j % 2][:, NB:2 * NB], ACT.Gelu,
                                     bias=bias[:, n + j:n + j + 1]).then_inc(stage.sem["gelu"], 1)
                if j:
                    high(j - 1)
            high(n - 1)
            if more:
                row_high(stage, m + 1)

        row_high(shared, 0)
        shared_blocks(act, lambda m, more: ffn(shared, m, bs1T, more))
        row_high(expert, 0)

        def biases_ready(e, u):
            act.wait_ge(w_split, (e + 1) * (2 * DT + 2))
            act.sem_inc(alone, 1)

        experts(act, biases_ready, lambda u, n: ffn(expert, n, b1[u], True))

    @block.vector
    def _(dve):
        steps = [0]

        def then(ins):
            steps[0] += 1
            ins.then_inc(link, 1)
            dve.wait_ge(link, steps[0])

        dve.wait_ge(s_free, 1)
        nc.vector.tensor_tensor(picks[:], keep["pick"][:, 0, :, :], keep["pick"][:, 1, :, :], ALU.add).then_inc(picks_ready, 1)
        dve.wait_ge(rank_mm, 1)
        then(nc.vector.tensor_copy(run[0][:, PAD:, :], psC[:, 0:NT * E].rearrange("p (t e) -> p t e", e=E)))
        at, shift = 0, 1
        while shift < NT:
            then(nc.vector.tensor_tensor(run[1 - at][:, PAD:, :], run[at][:, PAD:, :],
                                         run[at][:, PAD - shift:PAD - shift + NT, :], ALU.add))
            at, shift = 1 - at, 2 * shift
        then(nc.vector.tensor_scalar(counts[:], run[at][:, PAD + NT - 1, :], float(NB - 1), None, ALU.add))
        then(nc.vector.tensor_scalar(blocks_i[:], counts[:], NB.bit_length() - 1, None, ALU.logical_shift_right))
        then(nc.vector.tensor_copy(blocks[:], blocks_i[:]))
        then(nc.vector.tensor_tensor_scan(cum[:], ones_e[:], blocks[:], 0.0, ALU.mult, ALU.add))
        then(nc.vector.tensor_tensor(first[:], cum[:], blocks[:], ALU.subtract))
        nc.vector.tensor_copy(first_i[:, 0:E], first[:])
        then(nc.vector.tensor_copy(first_i[:, E:E + 1], cum[:, E - 1:E]))
        dve.sem_inc(table_ready, 1)
        then(nc.vector.tensor_scalar(first[:], first[:], float(NB), None, ALU.mult))
        then(nc.vector.tensor_tensor(place[:], psR[:, 0:NT * E].rearrange("p (t e) -> p t e", e=E),
                                     run[at][:, PAD - 1:PAD - 1 + NT, :], ALU.add))
        then(nc.vector.tensor_tensor(place[:], place[:], first[:].unsqueeze(1).to_broadcast([P, NT, E]), ALU.add))
        for k in range(2):
            then(nc.vector.tensor_tensor(picked[:], place[:], keep["pick"][:, k, :, :], ALU.mult))
            then(nc.vector.tensor_reduce(posf[:, k, :], picked[:], AX.X, ALU.add))
        nc.vector.tensor_copy(pos[:], posf[:]).then_inc(pos_ready, 1)
        dve.wait_ge(ratio_ready, 1)
        then(nc.vector.tensor_scalar(denom[:], ratio[:], 1.0, None, ALU.add))
        then(nc.vector.reciprocal(w[0][:], denom[:]))
        then(nc.vector.tensor_tensor(w[1][:], ratio[:], w[0][:], ALU.mult))

        def row_low(stage, m):
            stage.until(dve, "xh", of(stage, "xh", m, 1))
            nc.vector.tensor_tensor(xl[:].rearrange("p t n -> p (t n)"), psX[:], xh[:].rearrange("p t n -> p (t n)"),
                                    ALU.subtract).then_inc(stage.sem["xl"], 1)

        def ffn(stage, m, bias, more, result):
            n = stage.pairs

            def low(j):
                stage.until(dve, "acth", of(stage, "acth", m, j + 1))
                if j == 0:
                    stage.until(dve, "y_mm", of(stage, "y_mm", m))
                nc.vector.tensor_tensor(actl[:, j, :], actf[:, j % 2, :], acth[:, j, :], ALU.subtract)\
                    .then_inc(stage.sem["actl"], 1)

            for j in range(n):
                stage.until(dve, "actl", of(stage, "actl", m, j - 1))
                stage.until(dve, "gelu", of(stage, "gelu", m, j + 1))
                nc.vector.scalar_tensor_tensor(actf[:, j % 2, :], psH[j % 2][:, 0:NB], bias[:, j:j + 1],
                                               gel[:, j % 2, :], ALU.add, ALU.mult).then_inc(stage.sem["act"], 1)
                if j:
                    low(j - 1)
            low(n - 1)
            if more:
                row_low(stage, m + 1)
            stage.until(dve, "y_mm", of(stage, "y_mm", m, 1))
            result(m).then_inc(stage.sem["y_ready"], 1)

        def add_shared(m):
            for i in range(NBT):
                rows = keep["acc"][:, bass.ds(m * NBT + i, 1), :].rearrange("p o d -> p (o d)")
                ins = nc.vector.tensor_tensor(rows, psY[i][:, 0:D], rows, ALU.add)
            return ins

        row_low(shared, 0)
        shared_blocks(dve, lambda m, more: ffn(shared, m, bs1T, more, add_shared))
        row_low(expert, 0)

        def expert_rows(u):
            def rows(n):
                expert.until(dve, "y_stored", of(expert, "y_stored", n))
                for i in range(NBT):
                    ins = nc.vector.tensor_tensor(ysb[:, i, :], psY[i][:, 0:D], b2[u][:], ALU.add)
                return ins
            return rows

        def biases_ready(e, u):
            dve.wait_ge(w_split, (e + 1) * (2 * DT + 2))
            dve.sem_inc(alone, 1)

        experts(dve, biases_ready, lambda u, n: ffn(expert, n, b1[u], True, expert_rows(u)))
        for t in range(NT):
            dve.wait_ge(gathered[t % RING], 32 * (t // RING + 1))
            rows = keep["acc"][:, t, :]
            nc.vector.scalar_tensor_tensor(rows, yg[:, t % RING, 0, :], w[0][:, t:t + 1], rows, ALU.mult, ALU.add)\
                .then_inc(mix_link, 1)
            dve.wait_ge(mix_link, t + 1)
            nc.vector.scalar_tensor_tensor(rows, yg[:, t % RING, 1, :], w[1][:, t:t + 1], rows, ALU.mult, ALU.add)\
                .then_inc(mixed, 1)

    ctx.close()



def xattn_moe(nc, io):
    ctx = ExitStack()
    with ctx:
        keep, scratch = keep_tensors(nc, ctx), scratch_tensors(nc)
        fast = Path(nc, ctx, "fast", [TK // KC - 1], 2, False)
        whole = Path(nc, ctx, "whole", list(range(TK // KC)), 1, True, before=fast)
        shared, expert = Stage(nc, ctx, "shared", SH_PAIRS), Stage(nc, ctx, "expert", EX_PAIRS)
        setup(nc, ctx, io, keep, scratch, [fast, shared, expert])
        attention(nc, fast, io, keep, scratch)
        odd = nc.values_load(keep["odd_i"][0:1, 0:1], min_val=0, max_val=P)
        with nc.If(odd > 0):
            attention(nc, whole, io, keep, scratch)
        feed_forward(nc, io, keep, scratch, shared, expert)


_INS = dict(x="x", ctx="ctx_1024", mask="mask_BxSxS2_bk1", Wq="L0_xattn_Wq", bq="L0_xattn_bq", Wk="L0_xattn_Wk",
            bk="L0_xattn_bk", Wv="L0_xattn_Wv", bv="L0_xattn_bv", Wo="L0_xattn_Wo", bo="L0_xattn_bo",
            Ws1="L0_ffn_Ws1", bs1="L0_ffn_bs1", Ws2="L0_ffn_Ws2", bs2="L0_ffn_bs2", We1="L0_ffn_We1",
            be1="L0_ffn_be1", We2="L0_ffn_We2", be2="L0_ffn_be2", Wr="L0_ffn_Wr", br="L0_ffn_br")


def kernel(**inputs):
    import numpy as _np
    import concourse.bacc as _bacc
    from concourse import mybir as _mybir
    from concourse.bass_utils import run_bass_kernel_spmd as _run

    nc = _bacc.Bacc("TRN2", target_bir_lowering=False, num_devices=1)
    arrays, io = {}, {}
    for short, name in _INS.items():
        a = _np.ascontiguousarray(inputs[name])
        arrays[f"in_{name}_dram"] = a
        io[short] = nc.dram_tensor(f"in_{name}_dram", a.shape, _mybir.dt.from_np(a.dtype), kind="ExternalInput").ap()
    io["out"] = nc.dram_tensor("out_0_dram", (B, TQ, D), FP32, kind="ExternalOutput").ap()
    xattn_moe(nc, io)
    r = _run(nc, [arrays], core_ids=[0])
    return r.results[0]["out_0_dram"]
```

```python
import concourse.bass as bass
from concourse import mybir
from contextlib import ExitStack

FP32, FP16, BF16 = mybir.dt.float32, mybir.dt.float16, mybir.dt.bfloat16
I32, U32, U8 = mybir.dt.int32, mybir.dt.uint32, mybir.dt.uint8
ALU, ACT, AX = mybir.AluOpType, mybir.ActivationFunctionType, mybir.AxisListType

P = 128
B, TQ, TK, D = 8, 512, 1024, 256
H, DH = 16, 16
LEFT = 2
QT = TQ // P
DT = D // P
N = B * TQ
NT = N // P
KC = 256
NPAIR = H // 2
PARTS = 4
GROUPS = H // 4
E, HS, HR = 12, 512, 768
TAU = 1.5
EPS = 1e-5
MASKED = -60000.0
MASK_ROWS = 14
NEG = -1e30


class Path:

    ONCE = ("cleared", "extras", "began")
    LEFT_OVER = ("scattered", "rows_out")
    ONLY_MASKED = ("mask_loaded", "mask_ready", "negm", "odd_last")

    def __init__(self, nc, ctx, name, chunks, buffers, masked, before=None):
        self.name, self.chunks, self.buffers, self.masked = name, chunks, buffers, masked
        c = len(chunks)
        self.nc_ = c
        self.per = dict(
            x_loaded=16, ctx_loaded=16 * c, res_loaded=16, mask_loaded=16, mask_ready=1,
            ln1_link=2, ve1=1, rstd1=1, xn_ready=1, xT_mm=2, xTh=2, xTl=2, q_mm=2, qf=2, qh=2, ql=2,
            cT_mm=c, cTh=c, cTl=c, k_mm=c, kf=c, kh=c, kl=c, v_mm=c, v_ready=c,
            qstk_w=32, qs_loaded=128, kstk_w=32 * c, kz_loaded=(96 if masked else 128) * c,
            s_mm=32 * c, max_done=32 * c, negm=1, mT_mm=1, mT_ready=1, m_saved=16, m_rows=32,
            st_mm=32 * c, exp_done=32 * c, pv_mm=8 * c, oT_ready=4, oX_mm=4, rec=4, on_ready=4,
            onT_mm=2, onTh=2, onTl=2, o_mm=2, res_ready=1, x1_done=2, ln2_link=2, ve2=1, rstd2=1,
            xn2_ready=1, xn2_saved=16, acc_done=1, x2T_mm=2, x2h=2, x2l=2, r_mm=1, rt_link=5,
            picks_ready=1, rank_mm=1, place_link=5, scattered=16 * 2 * QT, rows_out=1, words_loaded=32, summed=QT - 1, odd_link=2,
            odd_last=1, worst=1, began=1, cleared=1, extras=16 * 2 * (buffers + max(buffers, c)))
        if before is None:
            self.passed = ctx.enter_context(nc.semaphore(f"{name}_passed"))
            self.sem = {n: ctx.enter_context(nc.semaphore(f"{name}_{n}")) for n in self.per}
            self.ahead = dict(self.per, scattered=0)
        else:
            self.passed, self.sem = before.passed, before.sem
            self.ahead = {n: before.ahead[n] + before.per[n] * (0 if n in self.ONLY_MASKED else 1 if n in self.ONCE else
                                                                B - LEFT if n in self.LEFT_OVER else B)
                          for n in self.per}

    def start_ahead(self, eng):
        for n, s in self.sem.items():
            if self.ahead[n]:
                eng.sem_inc(s, self.ahead[n])

    def until(self, eng, name, count, alone=False):
        if isinstance(count, int) and count <= 0:
            return
        eng.wait_ge(self.sem[name], count + self.ahead[name])
        if alone and not isinstance(count, int):
            eng.sem_inc(self.passed, 1)

    def of(self, name, b, k):
        return b * self.per[name] + k


MISC = dict(oX3=1, cT=0, xT0=1, xT1=0, onT0=1, onT1=0, oX0=1, K=0, Q0=1, Q1=0, O0=1, O1=0,
            mT=1, oX1=0, oX2=1, V=0, x2T0=1, x2T1=0, R=1, rank=1, odd=0)


def attention(nc, path, io, keep, scratch):
    ctx = ExitStack()
    C, NB, general = path.nc_, path.buffers, path.masked
    sem, until, of, sem_per = path.sem, path.until, path.of, path.per

    def sb(name, shape, dt):
        return ctx.enter_context(nc.sbuf_tensor(f"{path.name}_{name}", shape, dt))

    xbuf = sb("xbuf", [P, QT, D], FP32)
    xres = sb("xres", [P, QT, D], FP32)
    xn = sb("xn", [P, QT, D], FP32)
    stats = sb("stats", [P, QT, 6], FP32)
    mv = sb("mv", [P, QT, 2], FP32)
    rstd = sb("rstd", [P, QT], FP32)
    xTh = sb("xTh", [P, DT, TQ], FP16)
    xTl = sb("xTl", [P, DT, TQ], FP16)
    qf = sb("qf", [P, DT, TQ], FP32)
    qh = sb("qh", [P, DT, TQ], FP16)
    ql = sb("ql", [P, DT, TQ], FP16)
    cbuf = sb("cbuf", [P, 2, D], FP32)
    cTh = sb("cTh", [P, DT, KC], FP16)
    cTl = sb("cTl", [P, DT, KC], FP16)
    kf = sb("kf", [P, DT, KC], FP32)
    kh = sb("kh", [P, DT, KC], FP16)
    kl = sb("kl", [P, DT, KC], FP16)
    nk = max(NB, C)
    Qs = [sb(f"Qs{u}", [P, NPAIR, TQ], FP16) for u in range(NB)]
    Kz = [sb(f"Kz{u}", [P, NPAIR, 2, KC], FP16) for u in range(nk)]
    V = [sb(f"V{u}", [P, 2, H, 32], FP32) for u in range(nk)]
    NPT = 4 if general else 8
    PT = sb("PT", [P, NPT, TQ], FP32)
    mx = sb("mx", [P, QT, H, C], FP32)
    negm = sb("negm", [P, QT, H], FP32)
    mT16 = sb("mT16", [H, TQ], FP16)
    oT = sb("oT", [P, 2, TQ], FP32)
    rec = sb("rec", [P, QT, 4], FP32)
    if general:
        on = qf[:].rearrange("p o (u d) -> p (o u) d", d=D)
    else:
        on = sb("on", [P, QT, D], FP32)[:]
    onTh = sb("onTh", [P, DT, TQ], FP16)
    onTl = sb("onTl", [P, DT, TQ], FP16)
    xn2 = sb("xn2", [P, QT, D], FP32)
    stats2 = sb("stats2", [P, QT, 6], FP32)
    mv2 = sb("mv2", [P, QT, 2], FP32)
    rstd2 = sb("rstd2", [P, QT], FP32)
    x2h = sb("x2h", [P, DT, TQ], FP16)
    x2l = sb("x2l", [P, DT, TQ], FP16)
    lg = sb("lg", [P, QT, E], FP32)
    top = sb("top", [P, QT, 8], FP32)
    topi = sb("topi", [P, QT, 8], U32)
    topf = sb("topf", [P, QT, 2], FP32)
    picks = sb("picks", [P, QT, E], FP16)
    place = sb("place", [P, QT, E], FP32)
    picked = sb("picked", [P, 2, QT, E], FP32)
    posf = sb("posf", [P, 2, QT], FP32)
    pos = sb("pos", [P, 2, QT], I32)
    if not general:
        WORDS, LASTW = TK // 4, KC // 4
        words = sb("words", [P, QT, WORDS], I32)
        sums = sb("sums", [P, WORDS], I32)
        shown = sb("shown", [P, LASTW], I32)
        shown4 = sb("shown4", [P, LASTW], I32)
        diff = sb("diff", [P, WORDS], I32)
        worst = sb("worst", [P, WORDS], I32)
        most = sb("most", [P, 1], FP32)
        odd_row = sb("odd_row", [P, 1], FP32)
    if general:
        mask8 = sb("mask8", [P, QT, TK], U8)
        maskb = sb("maskb", [P, QT, TK], BF16)
    psS = [ctx.enter_context(nc.psum_tensor(f"{path.name}_psS{i}", [P, 512], FP32)) for i in range(2)]
    psT = [ctx.enter_context(nc.psum_tensor(f"{path.name}_psT{i}", [P, 512], FP32)) for i in range(2)]
    psV = [ctx.enter_context(nc.psum_tensor(f"{path.name}_psV{i}", [P, 512], FP32)) for i in range(2)]
    psM = [ctx.enter_context(nc.psum_tensor(f"{path.name}_psM{i}", [P, 512], FP32)) for i in range(2)]
    qstk, kstk = scratch["qstk"], scratch["kstk"]
    x_v = io["x"].rearrange("b (t p) d -> b p t d", p=P)
    c_v = io["ctx"].rearrange("b (c t p) d -> b c p t d", p=P, t=2)
    m_v = io["mask"].rearrange("b (t p) k -> b p t k", p=P)
    UNITS = 2 * C * GROUPS
    SCORES = (0, 4, 6, 6, 6, 6, 4, 0)

    def kv(u, c):
        return c if general else u

    def batches(eng, body):
        if general:
            with eng.Fori(0, B) as b:
                body(b, 0)
            return
        body(0, 0)
        body(1, 1)
        with eng.Fori(0, (B - 4) // 2) as pair:
            body(pair * 2 + 2, 0)
            body(pair * 2 + 3, 1)
        body(B - 2, 0)
        body(B - 1, 1)

    def first(b):
        return isinstance(b, int) and b == 0

    def left_over(b):
        return not general and isinstance(b, int) and b >= B - LEFT

    def early(b):
        return isinstance(b, int) and b < 2

    def follows(b, n):
        return not isinstance(b, int) or b + n < B

    nc.disable_value_cache = general
    block = ctx.enter_context(nc.Block())

    @block.sync
    def _(sp):
        def until_sp(name, count):
            until(sp, name, count, alone=True)

        def load_x(b):
            until_sp("xn_ready", of("xn_ready", b, 0))
            sp.dma_start(xbuf[:], x_v[b]).then_inc(sem["x_loaded"], 16)

        def load_ctx(b, i):
            until_sp("cT_mm", of("cT_mm", b, i))
            sp.dma_start(cbuf[:], c_v[b, path.chunks[i]]).then_inc(sem["ctx_loaded"], 16)

        def load_res(b):
            until_sp("acc_done", of("acc_done", b, 0))
            until_sp("xn2_ready", of("xn2_ready", b, 0))
            sp.dma_start(xres[:], x_v[b]).then_inc(sem["res_loaded"], 16)

        def write_q(b):
            until_sp("qs_loaded", of("qs_loaded", b, 0))
            for part, (tile, done) in enumerate(((qh, "qh"), (ql, "ql"))):
                until_sp(done, of(done, b, DT))
                sp.dma_start(qstk[part].rearrange("(o p) q -> p o q", p=P), tile[:]).then_inc(sem["qstk_w"], 16)

        def stack_q(b, u):
            until_sp("qstk_w", of("qstk_w", b, 32))
            until_sp("st_mm", of("st_mm", b - NB + 1, 0))
            for j in range(2):
                for s, part in enumerate((0, 1, 0)):
                    r = 64 * j + DH * s
                    src = qstk[part].rearrange("(t j r) q -> j r t q", j=2, r=DH)
                    sp.dma_start(Qs[u][r:r + DH, :, :], src[j]).then_inc(sem["qs_loaded"], 16)
                r = 64 * j + 48
                sp.dma_start(Qs[u][r:r + 1, :, :], scratch["zero_row"][:, 0:NPAIR, :]).then_inc(sem["qs_loaded"], 16)

        def write_k(b, i):
            n = sem_per["kz_loaded"] // C
            until_sp("kz_loaded", of("kz_loaded", b, n * i))
            for part, (tile, done) in enumerate(((kh, "kh"), (kl, "kl"))):
                until_sp(done, of(done, b, i + 1))
                sp.dma_start(kstk[part].rearrange("(o p) k -> p o k", p=P), tile[:]).then_inc(sem["kstk_w"], 16)

        def stack_k(b, u, i):
            until_sp("kstk_w", of("kstk_w", b, 32 * (i + 1)))
            until_sp("st_mm", of("st_mm", b - NB + 1, 0))
            for j in range(2):
                for s, part in enumerate((0, 0, 1)):
                    r = 64 * j + DH * s
                    src = kstk[part].rearrange("(t j r) k -> j r t k", j=2, r=DH)
                    sp.dma_start(Kz[kv(u, i)][r:r + DH, :, j, :], src[j]).then_inc(sem["kz_loaded"], 16)
                if not general:
                    r = 64 * j + 49
                    row = scratch["kmask"][bass.ds(b, 1), path.chunks[i] * KC:(path.chunks[i] + 1) * KC]
                    sp.dma_start(Kz[kv(u, i)][r:r + MASK_ROWS, :, j, :],
                                 row.unsqueeze(1).to_broadcast([MASK_ROWS, NPAIR, KC])).then_inc(sem["kz_loaded"], 16)

        def extra_rows():
            until_sp("cleared", 1)
            for j in range(2):
                r = 64 * j + 48
                for tile in Qs:
                    sp.dma_start(tile[r:r + DH, :, :], scratch["q_rows"].unsqueeze(1).to_broadcast([DH, NPAIR, TQ]))\
                        .then_inc(sem["extras"], 16)
                for tile in Kz:
                    sp.dma_start(tile[r:r + DH, :, j, :],
                                 scratch["k_rows"].unsqueeze(1).to_broadcast([DH, NPAIR, KC])).then_inc(sem["extras"], 16)

        def max_rows(b, u):
            until_sp("mT_ready", of("mT_ready", b, 1))
            until_sp("m_rows", of("m_rows", b, 0))
            sp.dma_start(scratch["max_rows"], mT16[:]).then_inc(sem["m_saved"], 16)
            until_sp("m_saved", of("m_saved", b, 16))
            for j in range(2):
                sp.dma_start(Qs[u][64 * j + 48:64 * j + 49, :, :],
                             scratch["max_rows"].rearrange("(o t j) q -> j o t q", j=2, o=1)[j])\
                    .then_inc(sem["m_rows"], 16)

        def save_xn2(b):
            until_sp("xn2_ready", of("xn2_ready", b, 1))
            sp.dma_start(keep["xn2"][:, bass.ds(b * QT, QT), :], xn2[:]).then_inc(sem["xn2_saved"], 16)

        def load_words(b):
            until_sp("odd_link", of("odd_link", b, 0))
            sp.dma_start(words[:].bitcast(U8), m_v[b]).then_inc(sem["words_loaded"], 16)
            sp.dma_start(shown[:].bitcast(U8), io["mask"][b, 0, TK - KC:TK].partition_broadcast(P))\
                .then_inc(sem["words_loaded"], 16)

        if general:
            extra_rows()
            until_sp("extras", sem_per["extras"])
            with sp.Fori(0, B) as b:
                until_sp("st_mm", of("st_mm", b, 0))
                sp.dma_start(mask8[:], m_v[b]).then_inc(sem["mask_loaded"], 16)
                load_x(b)
                for i in range(C):
                    load_ctx(b, i)
                    if i == 0:
                        load_res(b)
                        write_q(b)
                        stack_q(b, 0)
                    write_k(b, i)
                    stack_k(b, 0, i)
                max_rows(b, 0)
                save_xn2(b)
            until_sp("xn2_saved", of("xn2_saved", B, 0))
            return
        load_x(0)
        load_ctx(0, 0)
        extra_rows()
        load_x(1)
        load_ctx(1, 0)
        until_sp("extras", sem_per["extras"])
        for b in range(2):
            write_k(b, 0)
            write_q(b)
            stack_k(b, b, 0)
            stack_q(b, b)
        max_rows(0, 0)

        def slot(b, u):
            if follows(b, 2):
                load_x(b + 2)
                load_ctx(b + 2, 0)
            if not early(b):
                save_xn2(b - 2)
            if not first(b):
                load_res(b - 1)
            load_words(b)
            if follows(b, 2):
                write_k(b + 2, 0)
                write_q(b + 2)
            if follows(b, 1):
                max_rows(b + 1, 1 - u)
            if follows(b, 2):
                stack_k(b + 2, u, 0)
                stack_q(b + 2, u)
        batches(sp, slot)
        save_xn2(B - 2)
        load_res(B - 1)
        save_xn2(B - 1)
        until_sp("xn2_saved", of("xn2_saved", B, 0))

    @block.tensor
    def _(pe):
        held = [None, None]
        ahead = dict(b=None, u=0, n=0, left=0)

        def start_scores(b, u, n, count):
            ahead.update(b=b, u=u, n=n, left=count)

        def one_score():
            if ahead["left"]:
                scores(ahead["b"], ahead["u"], ahead["n"])
                ahead.update(n=ahead["n"] + 1, left=ahead["left"] - 1)

        def misc(what, b, reader, k=1):
            bank = MISC[what]
            if held[bank]:
                until(pe, *held[bank])
            held[bank] = (reader, of(reader, b, k))
            return psM[bank]

        def transposes(what, b, src, done, reader):
            for dt in range(DT):
                ps = misc(f"{what}{dt}", b, reader, dt + 1)
                for t in range(QT):
                    mm = nc.tensor.transpose(ps[:, t * P:(t + 1) * P], src[:, t, dt * P:(dt + 1) * P], keep["ident"][:])
                mm.then_inc(sem[done], 1)
                one_score()

        def split_product(out, left, right, cols):
            terms = [(left[0], right[0]), (left[0], right[1]), (left[1], right[0])]
            for dt in range(DT):
                if dt:
                    one_score()
                for n, (a, w) in enumerate(terms):
                    mm = nc.tensor.matmul(out, a(dt), w(dt), start=(dt == 0 and n == 0),
                                          stop=(dt == DT - 1 and n == 2))
            return mm

        def w_cols(w, part, lo, n):
            return lambda dt: keep[f"{w}{part}"][:, dt, lo:lo + n]

        def xT(b):
            until(pe, "xn_ready", of("xn_ready", b, 1))
            transposes("xT", b, xn, "xT_mm", "xTl")

        def cT(b, i):
            until(pe, "ctx_loaded", of("ctx_loaded", b, 16 * (i + 1)))
            ps = misc("cT", b, "cTl", i + 1)
            for dt in range(DT):
                for t in range(2):
                    mm = nc.tensor.transpose(ps[:, dt * KC + t * P:dt * KC + (t + 1) * P],
                                             cbuf[:, t, dt * P:(dt + 1) * P], keep["ident"][:])
            mm.then_inc(sem["cT_mm"], 1)

        def q_proj(b):
            until(pe, "xTl", of("xTl", b, 2))
            for o in range(DT):
                ps = misc(f"Q{o}", b, "qf", o + 1)
                split_product(ps[:], (w_cols("Wq", "h", o * P, P), w_cols("Wq", "l", o * P, P)),
                              (lambda dt: xTh[:, dt, :], lambda dt: xTl[:, dt, :]), TQ).then_inc(sem["q_mm"], 1)

        def k_proj(b, i):
            until(pe, "cTl", of("cTl", b, i + 1))
            ps = misc("K", b, "kf", i + 1)
            for o in range(DT):
                mm = split_product(ps[:, o * KC:(o + 1) * KC], (w_cols("Wk", "h", o * P, P), w_cols("Wk", "l", o * P, P)),
                                   (lambda dt: cTh[:, dt, :], lambda dt: cTl[:, dt, :]), KC)
            mm.then_inc(sem["k_mm"], 1)

        def v_proj(b, i):
            ps = misc("V", b, "v_ready", i + 1)
            for t in range(2):
                mm = split_product(ps[:, t * D:(t + 1) * D],
                                   (lambda dt: cTh[:, dt, t * P:(t + 1) * P], lambda dt: cTl[:, dt, t * P:(t + 1) * P]),
                                   (w_cols("Wv", "h", 0, D), w_cols("Wv", "l", 0, D)), D)
            mm.then_inc(sem["v_mm"], 1)

        def scores(b, u, n):
            t, p, c = n // (NPAIR * C), n // C % NPAIR, n % C
            until(pe, "max_done", of("max_done", b, n - 1))
            out = psS[n % 2]
            mm = nc.tensor.matmul(out[:], Qs[u][:, p, t * P:(t + 1) * P], Kz[kv(u, c)][:, p, :, :],
                                  start=True, stop=not general)
            if general:
                for j in range(2):
                    mm = nc.tensor.matmul(out[:, j * KC:(j + 1) * KC], keep["negI"][:],
                                          maskb[:, t, c * KC:(c + 1) * KC], start=False, stop=(j == 1))
            mm.then_inc(sem["s_mm"], 1)

        def stacks_ready(b):
            until(pe, "qs_loaded", of("qs_loaded", b + 1, 0))
            until(pe, "kz_loaded", of("kz_loaded", b + 1, 0))
            if first(b) or general:
                until(pe, "extras", sem_per["extras"])
            if general:
                until(pe, "mask_ready", of("mask_ready", b, 1))

        def mT(b):
            if C == 1:
                until(pe, "max_done", of("max_done", b, 32))
            else:
                until(pe, "negm", of("negm", b, 1))
            ps = misc("mT", b, "mT_ready")
            for t in range(QT):
                mm = nc.tensor.transpose(ps[0:H, t * P:(t + 1) * P], negm[:, t, :], keep["ident"][:])
            mm.then_inc(sem["mT_mm"], 1)

        def scores_T(b, u, n):
            g, kb, i = n // (8 * C), n // 4 % (2 * C), n % 4
            h = 4 * g + i
            if n == 0:
                until(pe, "m_rows", of("m_rows", b, 32))
            until(pe, "exp_done", of("exp_done", b, n - 1))
            out = psT[n % 2]
            mm = nc.tensor.matmul(out[:], Kz[kv(u, kb // 2)][:, h // 2, h % 2, (kb % 2) * P:(kb % 2 + 1) * P],
                                  Qs[u][:, h // 2, :], start=True, stop=not general)
            if general:
                for t in range(QT):
                    mm = nc.tensor.matmul(out[:, t * P:(t + 1) * P], maskb[:, t, kb * P:(kb + 1) * P],
                                          keep["negI"][:], start=False, stop=(t == QT - 1))
            mm.then_inc(sem["st_mm"], 1)

        def weighted(b, u, k):
            g, kb = k // (2 * C), k % (2 * C)
            until(pe, "exp_done", of("exp_done", b, 4 * k + 4))
            if k == 0:
                until(pe, "v_ready", of("v_ready", b, C))
            if kb == 0:
                until(pe, "oT_ready", of("oT_ready", b, g - 1))
            for i in range(4):
                mm = nc.tensor.matmul(psV[g % 2][32 * i:32 * i + 32, :], V[kv(u, kb // 2)][:, kb % 2, 4 * g + i, :],
                                      PT[:, (4 * k + i) % NPT, :], start=(kb == 0), stop=(kb == 2 * C - 1),
                                      skip_group_check=True)
            mm.then_inc(sem["pv_mm"], 1)

        def oX(b, g):
            until(pe, "oT_ready", of("oT_ready", b, g + 1))
            ps = misc(f"oX{g}", b, "on_ready", g + 1)
            for t in range(QT):
                mm = nc.tensor.transpose(ps[:, t * P:(t + 1) * P], oT[:, g % 2, t * P:(t + 1) * P], keep["ident"][:])
            mm.then_inc(sem["oX_mm"], 1)

        def onT(b):
            until(pe, "on_ready", of("on_ready", b, GROUPS))
            transposes("onT", b, on, "onT_mm", "onTl")

        def o_proj(b):
            until(pe, "onTl", of("onTl", b, 2))
            for k in range(2):
                ps = misc(f"O{k}", b, "x1_done", k + 1)
                for j in range(2):
                    lo = (2 * k + j) * P
                    mm = split_product(ps[:, j * D:(j + 1) * D],
                                       (lambda dt: onTh[:, dt, lo:lo + P], lambda dt: onTl[:, dt, lo:lo + P]),
                                       (w_cols("Wo", "h", 0, D), w_cols("Wo", "l", 0, D)), D)
                mm.then_inc(sem["o_mm"], 1)

        def x2T(b):
            until(pe, "xn2_ready", of("xn2_ready", b, 1))
            transposes("x2T", b, xn2, "x2T_mm", "x2l")

        def router(b):
            until(pe, "x2l", of("x2l", b, 2))
            ps = misc("R", b, "rt_link")
            for t in range(QT):
                mm = split_product(ps[:, t * E:(t + 1) * E],
                                   (lambda dt: x2h[:, dt, t * P:(t + 1) * P], lambda dt: x2l[:, dt, t * P:(t + 1) * P]),
                                   (w_cols("Wr", "h", 0, E), w_cols("Wr", "l", 0, E)), E)
            mm.then_inc(sem["r_mm"], 1)

        def rank(b):
            until(pe, "picks_ready", of("picks_ready", b, 1))
            ps = misc("rank", b, "place_link", 2)
            for t in range(QT + 1):
                for s in range(min(t + 1, QT)):
                    left = keep["below"] if s == t else keep["ones16"]
                    mm = nc.tensor.matmul(ps[:, t * E:(t + 1) * E], left[:], picks[:, s, :], start=(s == 0),
                                          stop=(s == min(t, QT - 1)))
            mm.then_inc(sem["rank_mm"], 1)

        def last_of(b):
            return [("x2l", of("x2l", b, 2)), ("place_link", of("place_link", b, 2))]

        if general:
            with pe.Fori(0, B) as b:
                held[:] = last_of(b - 1)
                xT(b)
                for i in range(C):
                    cT(b, i)
                    if i == 0:
                        q_proj(b)
                    k_proj(b, i)
                    v_proj(b, i)
                stacks_ready(b)
                for n in range(32 * C):
                    scores(b, 0, n)
                mT(b)
                for k in range(UNITS):
                    for i in range(4):
                        scores_T(b, 0, 4 * k + i)
                    weighted(b, 0, k)
                    if k % (2 * C) == 2 * C - 1:
                        oX(b, k // (2 * C))
                onT(b)
                o_proj(b)
                x2T(b)
                router(b)
                rank(b)
            return
        for b in range(2):
            xT(b)
            cT(b, 0)
            k_proj(b, 0)
            q_proj(b)
            v_proj(b, 0)
        stacks_ready(0)
        for n in range(32):
            scores(0, 0, n)
        mT(0)
        for bank in held:
            until(pe, *bank)

        def slot(b, u):
            if not isinstance(b, int) or b == B - 2:
                held[:] = [("x2l", of("x2l", b - 2, 2)), ("rt_link", of("rt_link", b - 2, 1))]
            for i in range(4):
                scores_T(b, u, i)
            for k in range(UNITS):
                if k == 1 and follows(b, 1):
                    stacks_ready(b + 1)
                if follows(b, 1):
                    start_scores(b + 1, 1 - u, sum(SCORES[:k]), SCORES[k])
                for i in range(4):
                    if k + 1 < UNITS:
                        scores_T(b, u, 4 * (k + 1) + i)
                    one_score()
                weighted(b, u, k)
                one_score()
                if k == 0 and not early(b):
                    rank(b - 2)
                if k == 0 and not first(b):
                    oX(b - 1, 3)
                if k == 0 and follows(b, 2):
                    cT(b + 2, 0)
                if k == 1 and follows(b, 2):
                    xT(b + 2)
                if k == 2 and not first(b):
                    onT(b - 1)
                if k == 3:
                    oX(b, 0)
                if k == 3 and follows(b, 2):
                    k_proj(b + 2, 0)
                if k == 4 and follows(b, 2):
                    q_proj(b + 2)
                if k == 5 and not first(b):
                    o_proj(b - 1)
                while ahead["left"]:
                    one_score()
                if k == 6 and follows(b, 1):
                    mT(b + 1)
                if k == 6:
                    oX(b, 1)
            oX(b, 2)
            if follows(b, 2):
                v_proj(b + 2, 0)
            if not first(b):
                x2T(b - 1)
                router(b - 1)
        batches(pe, slot)
        rank(B - 2)
        oX(B - 1, 3)
        onT(B - 1)
        o_proj(B - 1)
        x2T(B - 1)
        router(B - 1)
        until(pe, "odd_last", 2)
        nc.tensor.matmul(misc("odd", B - 1, "odd_last", 1)[0:1, 0:1], odd_row[:], keep["ones32"][:], start=True,
                         stop=True).then_inc(sem["odd_last"], 1)
        rank(B - 1)

    @block.scalar
    def _(act):
        def high(what, dst, b, after, done, n=DT):
            for dt in range(n):
                until(act, after, of(after, b, dt + 1))
                nc.scalar.activation(dst[:, dt, :], psM[MISC[f"{what}{dt}"]][:], ACT.Copy).then_inc(sem[done], 1)

        def xT_high(b):
            until(act, "q_mm", of("q_mm", b, 0))
            high("xT", xTh, b, "xT_mm", "xTh")

        def cT_high(b, i):
            until(act, "v_mm", of("v_mm", b, i))
            until(act, "cT_mm", of("cT_mm", b, i + 1))
            nc.scalar.activation(cTh[:].rearrange("p a k -> p (a k)"), psM[MISC["cT"]][:], ACT.Copy).then_inc(sem["cTh"], 1)

        def q_high(b):
            until(act, "qstk_w", of("qstk_w", b, 0))
            for o in range(DT):
                until(act, "qf", of("qf", b, o + 1))
                nc.scalar.activation(qh[:, o, :], qf[:, o, :], ACT.Copy).then_inc(sem["qh"], 1)

        def k_high(b, i):
            until(act, "kstk_w", of("kstk_w", b, 32 * i))
            until(act, "kf", of("kf", b, i + 1))
            nc.scalar.activation(kh[:].rearrange("p a k -> p (a k)"), kf[:].rearrange("p a k -> p (a k)"),
                                 ACT.Copy).then_inc(sem["kh"], 1)

        def max_T(b):
            until(act, "m_rows", of("m_rows", b, 0))
            until(act, "mT_mm", of("mT_mm", b, 1))
            nc.scalar.activation(mT16[:], psM[MISC["mT"]][0:H, :], ACT.Copy).then_inc(sem["mT_ready"], 1)

        def exps(b, k, these=range(4)):
            for i in these:
                n = 4 * k + i
                until(act, "st_mm", of("st_mm", b, n + 1))
                if i == 0:
                    until(act, "pv_mm", of("pv_mm", b, k + 1 - NPT // 4))
                nc.scalar.activation(PT[:, n % NPT, :], psT[n % 2][:], ACT.Exp).then_inc(sem["exp_done"], 1)

        def out_T(b, g):
            until(act, "oX_mm", of("oX_mm", b, g - 1))
            until(act, "pv_mm", of("pv_mm", b, 2 * C * (g + 1)))
            nc.scalar.activation(oT[:, g % 2, :], psV[g % 2][:], ACT.Copy).then_inc(sem["oT_ready"], 1)

        def onT_high(b):
            until(act, "o_mm", of("o_mm", b, 0))
            high("onT", onTh, b, "onT_mm", "onTh")

        def x2_high(b):
            until(act, "r_mm", of("r_mm", b, 0))
            high("x2T", x2h, b, "x2T_mm", "x2h")

        if general:
            with act.Fori(0, B) as b:
                xT_high(b)
                for i in range(C):
                    cT_high(b, i)
                    if i == 0:
                        q_high(b)
                    k_high(b, i)
                max_T(b)
                for k in range(UNITS):
                    exps(b, k)
                    if k % (2 * C) == 2 * C - 1:
                        out_T(b, k // (2 * C))
                onT_high(b)
                x2_high(b)
            return
        for b in range(2):
            xT_high(b)
            cT_high(b, 0)
            k_high(b, 0)
            q_high(b)
        max_T(0)

        def slot(b, u):
            for k in range(UNITS):
                exps(b, k, (0, 1))
                if k == 1 and follows(b, 2):
                    cT_high(b + 2, 0)
                if k == 2 and follows(b, 2):
                    xT_high(b + 2)
                if k == 3 and not first(b):
                    onT_high(b - 1)
                if k == 5 and follows(b, 2):
                    k_high(b + 2, 0)
                if k == 6 and follows(b, 2):
                    q_high(b + 2)
                exps(b, k, (2, 3))
                if k == 7 and follows(b, 1):
                    max_T(b + 1)
                if k in (2, 4, 6):
                    out_T(b, (k - 2) // 2)
            out_T(b, 3)
            if not first(b):
                x2_high(b - 1)
        batches(act, slot)
        onT_high(B - 1)
        x2_high(B - 1)

    @block.vector
    def _(dve):
        ahead = dict(b=None, n=0, left=0)

        def one_maximum():
            if ahead["left"]:
                maximum(ahead["b"], ahead["n"])
                ahead.update(n=ahead["n"] + 1, left=ahead["left"] - 1)

        def low(what, dst, hi, b, after, done):
            for dt in range(DT):
                until(dve, after, of(after, b, dt + 1))
                nc.vector.tensor_tensor(dst[:, dt, :], psM[MISC[f"{what}{dt}"]][:], hi[:, dt, :],
                                        ALU.subtract).then_inc(sem[done], 1)
                one_maximum()

        def moments(b, src, st, mom, link):
            for t in range(QT):
                ins = nc.vector.bn_stats(st[:, t, :], src[:, t, :])
            ins.then_inc(sem[link], 1)
            until(dve, link, of(link, b, 1), alone=True)
            for t in range(QT):
                ins = nc.vector.bn_aggr(mom[:, t, :], st[:, t, :])
            ins.then_inc(sem[link], 1)

        def normalise(src, mom, rs, dst):
            for t in range(QT):
                ins = nc.vector.tensor_scalar(dst[:, t, :], src[:, t, :], mom[:, t, 0:1], rs[:, t:t + 1],
                                              ALU.subtract, ALU.mult)
            return ins

        def ln1_moments(b):
            until(dve, "x_loaded", of("x_loaded", b, 16), alone=True)
            moments(b, xbuf, stats, mv, "ln1_link")

        def ln1(b):
            until(dve, "rstd1", of("rstd1", b, 1))
            until(dve, "xT_mm", of("xT_mm", b, 0))
            normalise(xbuf, mv, rstd, xn).then_inc(sem["xn_ready"], 1)

        def xT_low(b):
            until(dve, "q_mm", of("q_mm", b, 0))
            low("xT", xTl, xTh, b, "xTh", "xTl")

        def cT_low(b, i):
            until(dve, "cTh", of("cTh", b, i + 1))
            nc.vector.tensor_tensor(cTl[:].rearrange("p a k -> p (a k)"), psM[MISC["cT"]][:],
                                    cTh[:].rearrange("p a k -> p (a k)"), ALU.subtract).then_inc(sem["cTl"], 1)

        def q_bias(b):
            for o in range(DT):
                until(dve, "ql", of("ql", b - 1, o + 1))
                until(dve, "q_mm", of("q_mm", b, o + 1))
                nc.vector.tensor_scalar(qf[:, o, :], psM[MISC[f"Q{o}"]][:], keep["bqk"][:, o:o + 1], DH ** -0.5,
                                        ALU.add, ALU.mult).then_inc(sem["qf"], 1)

        def k_bias(b, i):
            until(dve, "kl", of("kl", b, i))
            until(dve, "k_mm", of("k_mm", b, i + 1))
            for o in range(DT):
                ins = nc.vector.tensor_scalar(kf[:, o, :], psM[MISC["K"]][:, o * KC:(o + 1) * KC],
                                              keep["bqk"][:, 2 + o:3 + o], None, ALU.add)
            ins.then_inc(sem["kf"], 1)

        def v_bias(b, u, i):
            until(dve, "pv_mm", of("pv_mm", b - NB + 1, 0))
            until(dve, "v_mm", of("v_mm", b, i + 1))
            for t in range(2):
                ins = nc.vector.tensor_tensor(V[kv(u, i)][:, t, :, 0:DH],
                                              psM[MISC["V"]][:, t * D:(t + 1) * D].rearrange("p (h r) -> p h r", h=H),
                                              keep["bv"][:].rearrange("p (h r) -> p h r", h=H), ALU.add)
            ins.then_inc(sem["v_ready"], 1)

        def maximum(b, n):
            t, p, c = n // (NPAIR * C), n // C % NPAIR, n % C
            until(dve, "s_mm", of("s_mm", b, n + 1))
            if n == 0:
                until(dve, "mT_mm", of("mT_mm", b, 0))
            src = psS[n % 2][:].rearrange("p (j k) -> p j k", j=2)
            if C == 1:
                nc.vector.tensor_reduce(negm[:, t, 2 * p:2 * p + 2], src, AX.X, ALU.max,
                                        negate=True).then_inc(sem["max_done"], 1)
            else:
                nc.vector.tensor_reduce(mx[:, t, 2 * p:2 * p + 2, c], src, AX.X, ALU.max).then_inc(sem["max_done"], 1)

        def row_max(b):
            if C > 1:
                until(dve, "max_done", of("max_done", b, 32 * C))
                nc.vector.tensor_reduce(negm[:].rearrange("p t h -> p (t h)"), mx[:].rearrange("p t h c -> p (t h) c"),
                                        AX.X, ALU.max, negate=True).then_inc(sem["negm"], 1)

        def normalised_out(b, g):
            k = MISC[f"oX{g}"]
            until(dve, "oX_mm", of("oX_mm", b, g + 1))
            src = psM[k][:].rearrange("p (t i r) -> p t i r", t=QT, i=4)
            until(dve, "on_ready", of("on_ready", b, g))
            nc.vector.reciprocal(rec[:], src[:, :, :, DH]).then_inc(sem["rec"], 1)
            until(dve, "rec", of("rec", b, g + 1))
            if g == 0:
                until(dve, "onT_mm", of("onT_mm", b, 0))
            dst = on.rearrange("p t (h r) -> p t h r", h=H)[:, :, 4 * g:4 * g + 4, :]
            nc.vector.tensor_tensor(dst, src[:, :, :, 0:DH], rec[:].unsqueeze(3).to_broadcast([P, QT, 4, DH]),
                                    ALU.mult).then_inc(sem["on_ready"], 1)

        def onT_low(b):
            until(dve, "o_mm", of("o_mm", b, 0))
            low("onT", onTl, onTh, b, "onTh", "onTl")

        def residual(b):
            until(dve, "res_ready", of("res_ready", b, 1))
            for k in range(2):
                until(dve, "o_mm", of("o_mm", b, k + 1))
                dst = xres[:, 2 * k:2 * k + 2, :].rearrange("p t d -> p (t d)")
                nc.vector.tensor_tensor(dst, psM[MISC[f"O{k}"]][:], dst, ALU.add).then_inc(sem["x1_done"], 1)

        def ln2_moments(b):
            until(dve, "x1_done", of("x1_done", b, 2), alone=True)
            moments(b, xres, stats2, mv2, "ln2_link")

        def ln2(b):
            until(dve, "rstd2", of("rstd2", b, 1))
            until(dve, "x2T_mm", of("x2T_mm", b, 0))
            until(dve, "xn2_saved", of("xn2_saved", b, 0))
            if not left_over(b - 1):
                until(dve, "rows_out", of("rows_out", b, 0))
            normalise(xres, mv2, rstd2, xn2).then_inc(sem["xn2_ready"], 1)

        def x2_low(b):
            until(dve, "r_mm", of("r_mm", b, 0))
            low("x2T", x2l, x2h, b, "x2h", "x2l")

        def route(b):
            until(dve, "r_mm", of("r_mm", b, 1))
            until(dve, "rt_link", of("rt_link", b, 0))
            nc.vector.tensor_tensor(lg[:], psM[MISC["R"]][:, 0:QT * E].rearrange("p (t e) -> p t e", t=QT),
                                    keep["br"][:].unsqueeze(1).to_broadcast([P, QT, E]), ALU.add).then_inc(sem["rt_link"], 1)
            until(dve, "rt_link", of("rt_link", b, 1), alone=True)
            for t in range(QT):
                ins = nc.vector.max(top[:, t, :], lg[:, t, :])
            ins.then_inc(sem["rt_link"], 1)
            until(dve, "rt_link", of("rt_link", b, 2), alone=True)
            for t in range(QT):
                ins = nc.vector.max_index(topi[:, t, :], top[:, t, :], lg[:, t, :])
            ins.then_inc(sem["rt_link"], 1)
            until(dve, "rt_link", of("rt_link", b, 3))
            nc.vector.tensor_copy(topf[:], topi[:, :, 0:2]).then_inc(sem["rt_link"], 1)
            nc.vector.tensor_tensor(keep["gap"][:, bass.ds(b * QT, QT)], top[:, :, 1], top[:, :, 0], ALU.subtract)
            until(dve, "rt_link", of("rt_link", b, 4))
            for k in range(2):
                ins = nc.vector.tensor_tensor(keep["pick"][:, k, bass.ds(b * QT, QT), :],
                                              keep["iota_e"][:].unsqueeze(1).to_broadcast([P, QT, E]),
                                              topf[:, :, k:k + 1].to_broadcast([P, QT, E]), ALU.is_equal)
            ins.then_inc(sem["rt_link"], 1)
            until(dve, "rt_link", of("rt_link", b, 5))
            until(dve, "rank_mm", of("rank_mm", b, 0))
            nc.vector.tensor_tensor(picks[:], keep["pick"][:, 0, bass.ds(b * QT, QT), :],
                                    keep["pick"][:, 1, bass.ds(b * QT, QT), :], ALU.add).then_inc(sem["picks_ready"], 1)

        def places(b):
            until(dve, "rank_mm", of("rank_mm", b, 1))
            ranks = psM[MISC["rank"]]
            nc.vector.tensor_tensor(place[:], ranks[:, 0:QT * E].rearrange("p (t e) -> p t e", t=QT),
                                    keep["next_row"][:].unsqueeze(1).to_broadcast([P, QT, E]), ALU.add)\
                .then_inc(sem["place_link"], 1)
            until(dve, "place_link", of("place_link", b, 1))
            nc.vector.tensor_tensor(keep["next_row"][:], ranks[:, QT * E:(QT + 1) * E], keep["next_row"][:], ALU.add)\
                .then_inc(sem["place_link"], 1)
            for k in range(2):
                ins = nc.vector.tensor_tensor(picked[:, k, :, :], place[:], keep["pick"][:, k, bass.ds(b * QT, QT), :], ALU.mult)
            ins.then_inc(sem["place_link"], 1)
            until(dve, "place_link", of("place_link", b, 3))
            nc.vector.tensor_reduce(posf[:].rearrange("p k t -> p (k t)"), picked[:].rearrange("p k t e -> p (k t) e"),
                                    AX.X, ALU.add).then_inc(sem["place_link"], 1)
            until(dve, "place_link", of("place_link", b, 4))
            nc.vector.tensor_copy(keep["row"][:, :, bass.ds(b * QT, QT)], posf[:])
            if left_over(b):
                until(dve, "place_link", of("place_link", b, 4), alone=True)
                dve.sem_inc(sem["place_link"], 1)
                return
            until(dve, "rows_out", of("rows_out", b, 0))
            nc.vector.tensor_copy(pos[:], posf[:]).then_inc(sem["place_link"], 1)

        def odd_keys(b):
            until(dve, "words_loaded", of("words_loaded", b, 32))
            nc.vector.tensor_scalar(shown4[:], shown[:], 2, None, ALU.logical_shift_left).then_inc(sem["odd_link"], 1)
            until(dve, "summed", of("summed", b, QT - 1))
            until(dve, "odd_link", of("odd_link", b, 1), alone=True)
            nc.vector.tensor_scalar(diff[:, 0:WORDS - LASTW], sums[:, 0:WORDS - LASTW], QT * 0x01010101, None,
                                    ALU.bitwise_xor)
            nc.vector.tensor_tensor(diff[:, WORDS - LASTW:], sums[:, WORDS - LASTW:], shown4[:], ALU.bitwise_xor)\
                .then_inc(sem["odd_link"], 1)
            until(dve, "odd_link", of("odd_link", b, 2))
            nc.vector.tensor_tensor(worst[:], worst[:], diff[:], ALU.bitwise_or).then_inc(sem["worst"], 1)
            until(dve, "worst", of("worst", b, 1))

        nc.vector.tensor_copy(keep["next_row"][:], keep["region"][:]).then_inc(sem["began"], 1)
        until(dve, "began", 1)
        if general:
            with dve.Fori(0, B) as b:
                until(dve, "mask_loaded", of("mask_loaded", b, 16))
                until(dve, "st_mm", of("st_mm", b, 0))
                nc.vector.tensor_copy(maskb[:], mask8[:]).then_inc(sem["mask_ready"], 1)
                ln1_moments(b)
                ln1(b)
                xT_low(b)
                for i in range(C):
                    cT_low(b, i)
                    if i == 0:
                        q_bias(b)
                    k_bias(b, i)
                    v_bias(b, 0, i)
                for n in range(32 * C):
                    maximum(b, n)
                row_max(b)
                for g in range(GROUPS):
                    normalised_out(b, g)
                onT_low(b)
                residual(b)
                ln2_moments(b)
                ln2(b)
                x2_low(b)
                route(b)
                places(b)
            return
        for b in range(2):
            ln1_moments(b)
            ln1(b)
            xT_low(b)
            cT_low(b, 0)
            k_bias(b, 0)
            q_bias(b)
            v_bias(b, b, 0)
        for n in range(32):
            maximum(0, n)
        until(dve, "cleared", 1)

        def slot(b, u):
            if follows(b, 2):
                ln1_moments(b + 2)
            for k in range(UNITS):
                if follows(b, 1):
                    ahead.update(b=b + 1, n=sum(SCORES[:k]), left=SCORES[k])
                for i in range(4 if k > 1 else 0):
                    one_maximum()
                between(b, k)
                while ahead["left"]:
                    one_maximum()
            normalised_out(b, 2)
            if follows(b, 2):
                v_bias(b + 2, u, 0)
            if not first(b):
                x2_low(b - 1)
                route(b - 1)

        def between(b, k):
            if k == 1:
                if not early(b):
                    places(b - 2)
                if follows(b, 2):
                    ln1(b + 2)
                if not first(b):
                    normalised_out(b - 1, 3)
                if follows(b, 2):
                    cT_low(b + 2, 0)
            if k == 2 and follows(b, 2):
                xT_low(b + 2)
            if k == 3 and not first(b):
                onT_low(b - 1)
            if k == 4:
                normalised_out(b, 0)
                one_maximum()
                if follows(b, 2):
                    k_bias(b + 2, 0)
            if k == 5 and follows(b, 2):
                q_bias(b + 2)
            if k == 6 and not first(b):
                residual(b - 1)
                ln2_moments(b - 1)
            if k == 7:
                normalised_out(b, 1)
                if not first(b):
                    ln2(b - 1)
                odd_keys(b)

        batches(dve, slot)
        places(B - 2)
        normalised_out(B - 1, 3)
        onT_low(B - 1)
        residual(B - 1)
        ln2_moments(B - 1)
        ln2(B - 1)
        x2_low(B - 1)
        nc.vector.tensor_reduce(most[:], worst[:], AX.X, ALU.max).then_inc(sem["odd_last"], 1)
        until(dve, "odd_last", 1)
        nc.vector.tensor_scalar(odd_row[:], most[:], 0.0, None, ALU.not_equal).then_inc(sem["odd_last"], 1)
        route(B - 1)
        until(dve, "odd_last", 3)
        nc.vector.tensor_copy(keep["odd_i"][:], psM[MISC["odd"]][0:1, 0:1])
        places(B - 1)

    @block.gpsimd
    def _(pool):
        def rstd_of(b, mom, link, rs, done, half):
            until(pool, link, of(link, b, 2))
            until(pool, done, of(done, b, 0), alone=True)
            nc.gpsimd.tensor_scalar(rs[:], mom[:, :, 1], EPS, None, ALU.add).then_inc(sem[half], 1)
            until(pool, half, of(half, b, 1))
            nc.gpsimd.tensor_tensor(rs[:], rs[:], keep["minus_half"][:], ALU.pow).then_inc(sem[done], 1)

        def q_low(b):
            until(pool, "qstk_w", of("qstk_w", b, 0))
            for o in range(DT):
                until(pool, "qh", of("qh", b, o + 1))
                nc.gpsimd.tensor_tensor(ql[:, o, :], qf[:, o, :], qh[:, o, :], ALU.subtract).then_inc(sem["ql"], 1)

        def k_low(b, i):
            until(pool, "kstk_w", of("kstk_w", b, 32 * i))
            until(pool, "kh", of("kh", b, i + 1))
            nc.gpsimd.tensor_tensor(kl[:].rearrange("p a k -> p (a k)"), kf[:].rearrange("p a k -> p (a k)"),
                                    kh[:].rearrange("p a k -> p (a k)"), ALU.subtract).then_inc(sem["kl"], 1)

        def res_bias(b):
            until(pool, "res_loaded", of("res_loaded", b, 16))
            for t in range(QT):
                ins = nc.gpsimd.tensor_tensor(xres[:, t, :], xres[:, t, :], keep["bo"][:], ALU.add)
            ins.then_inc(sem["res_ready"], 1)

        def keep_x1(b):
            until(pool, "x1_done", of("x1_done", b, 2))
            for t in range(QT):
                ins = nc.gpsimd.tensor_tensor(keep["acc"][:, bass.ds(b * QT + t, 1), :].rearrange("p o d -> p (o d)"),
                                              xres[:, t, :], keep["bs2"][:], ALU.add)
            ins.then_inc(sem["acc_done"], 1)

        def scatter(b):
            until(pool, "place_link", of("place_link", b, 5), alone=True)
            for t in range(QT):
                for k in range(2):
                    pool.indirect_dma_start(out=scratch["xs"][:, :],
                                            out_offset=bass.IndirectOffsetOnAxis(ap=pos[:, k, t:t + 1], axis=0),
                                            in_=xn2[:, t, :], in_offset=None, bounds_check=X_ROWS - 1)\
                        .then_inc(sem["scattered"], 16)

        def rows_out(b):
            until(pool, "scattered", of("scattered", b + 1, 0))
            pool.sem_inc(sem["rows_out"], 1)

        def sum_words(b):
            until(pool, "words_loaded", of("words_loaded", b, 32))
            nc.gpsimd.tensor_tensor(sums[:], words[:, 0, :], words[:, 1, :], ALU.add).then_inc(sem["summed"], 1)
            for t in range(2, QT):
                until(pool, "summed", of("summed", b, t - 1))
                nc.gpsimd.tensor_tensor(sums[:], sums[:], words[:, t, :], ALU.add).then_inc(sem["summed"], 1)

        def rstd1(b):
            rstd_of(b, mv, "ln1_link", rstd, "rstd1", "ve1")

        def rstd2_(b):
            rstd_of(b, mv2, "ln2_link", rstd2, "rstd2", "ve2")

        if not general:
            nc.gpsimd.memset(worst[:], 0)
        for tile in Kz:
            nc.gpsimd.memset(tile[:], 0.0)
        for tile in V:
            nc.gpsimd.memset(tile[:, :, :, DH + 1:32], 0.0)
            ins = nc.gpsimd.memset(tile[:, :, :, DH:DH + 1], 1.0)
        ins.then_inc(sem["cleared"], 1)
        if general:
            with pool.Fori(0, B) as b:
                rstd1(b)
                q_low(b)
                for i in range(C):
                    k_low(b, i)
                res_bias(b)
                rstd2_(b)
                keep_x1(b)
                scatter(b)
                rows_out(b)
            return
        for b in range(2):
            rstd1(b)
            k_low(b, 0)
            q_low(b)

        def slot(b, u):
            if follows(b, 2):
                rstd1(b + 2)
            if not early(b):
                scatter(b - 2)
            sum_words(b)
            if not first(b):
                res_bias(b - 1)
            if follows(b, 2):
                k_low(b + 2, 0)
            if follows(b, 2):
                q_low(b + 2)
            if not early(b):
                rows_out(b - 2)
            if not first(b):
                rstd2_(b - 1)
            if not first(b):
                keep_x1(b - 1)
        batches(pool, slot)
        res_bias(B - 1)
        rstd2_(B - 1)
        keep_x1(B - 1)

    nc.disable_value_cache = False
    ctx.close()


def setup(nc, ctx, io, keep, scratch, path_list):
    inner = ExitStack()

    def sb(name, shape, dt):
        return inner.enter_context(nc.sbuf_tensor(f"setup_{name}", shape, dt))

    def sem(name):
        return ctx.enter_context(nc.semaphore(f"setup_{name}"))

    names = ["Wq", "Wk", "Wv", "Wo"]
    raw = [sb(f"raw{w}", [P, DT, D], FP32) for w in names]
    raw_r = sb("rawWr", [P, DT, E], FP32)
    raw_b = sb("raw_b", [4, P], FP32)
    mask_row = sb("mask_row", [B, TK], U8)
    kmask = sb("kmask", [B, TK], FP16)
    rows = sb("rows", [DH, 1024], FP16)
    region_i = sb("region_i", [P, E], I32)
    psA = [inner.enter_context(nc.psum_tensor(f"setup_ps{i}", [P, 512], FP32)) for i in range(2)]
    loaded, consts, w_mm, w_high, w_low = sem("loaded"), sem("consts"), sem("w_mm"), sem("w_high"), sem("w_low")
    link, stored, dve_link = sem("link"), sem("stored"), sem("dve_link")
    small = sem("small")
    block = inner.enter_context(nc.Block())

    @block.sync
    def _(sp):
        for i, w in enumerate(names):
            sp.dma_start(raw[i][:], io[w].rearrange("(o p) d -> p o d", p=P)).then_inc(loaded, 16)
        sp.dma_start(raw_r[:], io["Wr"].rearrange("(t p) e -> p t e", p=P)).then_inc(small, 16)
        sp.dma_start(mask_row[:], io["mask"][:, 0, :]).then_inc(small, 16)
        for i, v in enumerate(("bq", "bk")):
            sp.dma_start(raw_b[2 * i:2 * i + 2, :], io[v].rearrange("(o p) -> o p", p=P)).then_inc(small, 16)
        for v in ("bv", "bo", "bs2", "br"):
            sp.dma_start(keep[v][:], io[v].partition_broadcast(P)).then_inc(small, 16)
        sp.wait_ge(dve_link, 1)
        sp.dma_start(scratch["kmask"], kmask[:]).then_inc(stored, 16)
        sp.wait_ge(consts, 1)
        sp.dma_start(scratch["q_rows"], rows[:, 0:512]).then_inc(stored, 16)
        sp.dma_start(scratch["k_rows"], rows[:, 512:512 + KC]).then_inc(stored, 16)
        sp.dma_start(scratch["zero_row"], rows[1:2, 512:1024].unsqueeze(1).to_broadcast([1, NPAIR, TQ]))\
            .then_inc(stored, 16)
        sp.wait_ge(small, 16 * 8)
        sp.wait_ge(stored, 64)

    @block.gpsimd
    def _(pool):
        nc.gpsimd.memset(rows[:, 0:512], 1.0)
        nc.gpsimd.memset(rows[:, 512:1024], 0.0).then_inc(link, 1)
        pool.wait_ge(link, 1)
        nc.gpsimd.memset(rows[0:1, 0:512], 0.0)
        nc.gpsimd.memset(rows[0:1, 512:512 + KC], 1.0).then_inc(consts, 1)
        nc.gpsimd.memset(keep["minus_half"][:], -0.5)
        nc.gpsimd.iota(region_i[:], pattern=[[REGION, E]], base=0, channel_multiplier=0).then_inc(link, 1)
        nc.gpsimd.memset(keep["ones16"][:], 1.0)
        nc.gpsimd.memset(keep["ones32"][:], 1.0)
        nc.gpsimd.memset(keep["ident"][:], 0.0).then_inc(link, 1)
        nc.gpsimd.iota(keep["iota_i"][:], pattern=[[1, E]], base=0, channel_multiplier=0).then_inc(link, 1)
        pool.wait_ge(link, 4)
        nc.gpsimd.affine_select(out=keep["ident"][:], in_=keep["ident"][:], compare_op=ALU.not_equal, fill=1.0,
                                base=0, pattern=[[-1, P]], channel_multiplier=1).then_inc(consts, 1)
        nc.gpsimd.affine_select(out=keep["below"][:], in_=keep["ones16"][:], compare_op=ALU.is_gt, fill=0.0,
                                base=0, pattern=[[1, P]], channel_multiplier=-1)
        nc.gpsimd.tensor_copy(keep["iota_e"][:], keep["iota_i"][:])
        nc.gpsimd.tensor_copy(keep["region"][:], region_i[:])
        pool.wait_ge(consts, 2)
        nc.gpsimd.tensor_scalar(keep["negI"][:], keep["ident"][:], NEG, None, ALU.mult)

    @block.tensor
    def _(pe):
        for path in path_list:
            path.start_ahead(pe)
        pe.wait_ge(consts, 2)
        pe.wait_ge(loaded, 16 * 4)
        for i in range(4):
            if i >= 2:
                pe.wait_ge(w_low, i - 1)
            for dt in range(DT):
                for o in range(DT):
                    mm = nc.tensor.transpose(psA[i % 2][:, dt * D + o * P:dt * D + (o + 1) * P],
                                             raw[i][:, o, dt * P:(dt + 1) * P], keep["ident"][:])
            mm.then_inc(w_mm, 1)
        pe.wait_ge(small, 16 * 8)
        pe.wait_ge(w_low, 3)
        nc.tensor.transpose(psA[0][:, 0:4], raw_b[:], keep["ident"][0:4, 0:4]).then_inc(w_mm, 1)

    @block.scalar
    def _(act):
        for i, w in enumerate(names):
            act.wait_ge(w_mm, i + 1)
            nc.scalar.activation(keep[f"{w}h"][:].rearrange("p a d -> p (a d)"), psA[i % 2][:], ACT.Copy).then_inc(w_high, 1)
        act.wait_ge(w_mm, 5)
        nc.scalar.activation(keep["bqk"][:], psA[0][:, 0:4], ACT.Copy)
        act.wait_ge(small, 16 * 8)
        nc.scalar.activation(keep["Wrh"][:], raw_r[:], ACT.Copy).then_inc(w_high, 1)

    @block.vector
    def _(dve):
        dve.wait_ge(small, 16 * 8)
        nc.vector.tensor_scalar(kmask[:], mask_row[:], MASKED, None, ALU.mult).then_inc(dve_link, 1)
        for i, w in enumerate(names):
            dve.wait_ge(w_high, i + 1)
            nc.vector.tensor_tensor(keep[f"{w}l"][:].rearrange("p a d -> p (a d)"), psA[i % 2][:],
                                    keep[f"{w}h"][:].rearrange("p a d -> p (a d)"), ALU.subtract).then_inc(w_low, 1)
        dve.wait_ge(w_high, 5)
        nc.vector.tensor_tensor(keep["Wrl"][:], raw_r[:], keep["Wrh"][:], ALU.subtract)

    inner.close()


def keep_tensors(nc, ctx):
    def sb(name, shape, dt):
        return ctx.enter_context(nc.sbuf_tensor(name, shape, dt))
    keep = {}
    for w, n in (("Wq", D), ("Wk", D), ("Wv", D), ("Wo", D), ("Wr", E)):
        for part in "hl":
            keep[w + part] = sb(w + part, [P, DT, n], FP16)
    keep["bqk"] = sb("bqk", [P, 4], FP32)
    for v, n in (("bv", D), ("bo", D), ("bs2", D), ("br", E)):
        keep[v] = sb(v, [P, n], FP32)
    keep["ident"] = sb("ident", [P, P], FP32)
    keep["negI"] = sb("negI", [P, P], BF16)
    keep["ones16"] = sb("ones16", [P, P], FP16)
    keep["ones32"] = sb("ones32", [P, 1], FP32)
    keep["below"] = sb("below", [P, P], FP16)
    keep["region"] = sb("region", [P, E], FP32)
    keep["next_row"] = sb("next_row", [P, E], FP32)
    keep["row"] = sb("row", [P, 2, NT], FP32)
    keep["iota_i"] = sb("iota_i", [P, E], I32)
    keep["iota_e"] = sb("iota_e", [P, E], FP32)
    keep["minus_half"] = sb("minus_half", [P, QT], FP32)
    keep["acc"] = sb("acc", [P, NT, D], FP32)
    keep["xn2"] = sb("xn2", [P, NT, D], FP32)
    keep["gap"] = sb("gap", [P, NT], FP32)
    keep["odd_i"] = sb("odd_i", [1, 1], I32)
    keep["pick"] = sb("pick", [P, 2, NT, E], FP16)
    return keep


def scratch_tensors(nc):
    def dram(name, shape, dt):
        return nc.dram_tensor(name, shape, dt).ap()
    return dict(qstk=dram("qstk", [2, D, TQ], FP16), kstk=dram("kstk", [2, D, KC], FP16),
                xs=dram("expert_in", [X_ROWS, D], FP32), ys=dram("expert_out", [ROWS, D], FP32),
                max_rows=dram("max_rows", [H, TQ], FP16), kmask=dram("kmask_rows", [B, TK], FP16), q_rows=dram("q_rows", [DH, TQ], FP16),
                k_rows=dram("k_rows", [DH, KC], FP16), zero_row=dram("zero_row", [1, NPAIR, TQ], FP16))


NB = 256
NBT = NB // P
NBLK = (2 * N + E * (NB - 1)) // NB
ROWS = NBLK * NB
REGION = N + NB
X_ROWS = E * REGION + NB
FIRST_SHARED = 8
FEW = 4
SH_PAIRS, EX_PAIRS = HS // P, HR // P


class Stage:

    def __init__(self, nc, ctx, name, pairs):
        self.pairs = pairs
        self.per = dict(x_loaded=16, xT_mm=1, xh=1, xl=1, h_mm=pairs, gelu=pairs, act=pairs, acth=pairs,
                        actl=pairs, y_mm=1, y_ready=1, y_stored=16)
        self.ahead = dict(self.per)
        self.passed = ctx.enter_context(nc.semaphore(f"{name}_passed"))
        self.sem = {n: ctx.enter_context(nc.semaphore(f"{name}_{n}")) for n in self.per}

    start_ahead, until, of = Path.start_ahead, Path.until, Path.of


def feed_forward(nc, io, keep, scratch, shared, expert):
    ctx = ExitStack()

    def sb(name, shape, dt):
        return ctx.enter_context(nc.sbuf_tensor(f"ff_{name}", shape, dt))

    def semaphore(name):
        return ctx.enter_context(nc.semaphore(f"ff_{name}"))

    counts = sb("counts", [P, E], FP32)
    counts_i = sb("counts_i", [P, E], I32)
    blocks_i = sb("blocks_i", [P, E], I32)
    blocks = sb("blocks", [P, E], FP32)
    ones_e = sb("ones_e", [P, E], FP32)
    cum = sb("cum", [P, E], FP32)
    first = sb("first", [P, E], FP32)
    first_i = sb("first_i", [P, E + 1], I32)
    ends_i = sb("ends_i", [P, E], I32)
    beyond = sb("beyond", [P, E], FP32)
    number_i = sb("number_i", [P, NBLK + 1], I32)
    number = sb("number", [P, NBLK + 1], FP32)
    past = sb("past", [P, NBLK + 1, E], FP32)
    start = sb("start", [P, NBLK + 1], FP32)
    start_i = sb("start_i", [P, NBLK + 1], I32)
    shift = sb("shift", [P, E], FP32)
    picked = sb("picked", [P, 2, NT, E], FP32)
    posf = sb("posf", [P, 2, NT], FP32)
    pos = sb("pos", [P, 2, NT], I32)
    last_pos = sb("last_pos", [P, 2, LEFT * QT], I32)
    ratio = sb("ratio", [P, NT], FP32)
    denom = sb("denom", [P, NT], FP32)
    w = [sb(f"w{k}", [P, NT], FP32) for k in range(2)]
    zeros = sb("zeros", [P, NBT, D], FP32)
    b_raw = sb("b_raw", [P, 3, P], FP32)
    b1T = sb("b1T", [P, 2 * EX_PAIRS * E], FP32)
    bs1T = sb("bs1T", [P, 2 * SH_PAIRS], FP32)
    st1 = sb("st1", [P, DT, 2 * HR], FP32)
    st2 = sb("st2", [P, EX_PAIRS, D], FP32)
    s1 = [sb(f"s1{x}", [P, DT, 2 * HS], FP16) for x in "hl"]
    s2 = [sb(f"s2{x}", [P, SH_PAIRS, D], FP16) for x in "hl"]
    w1 = [[sb(f"w1{x}{u}", [P, DT, 2 * HR], FP16) for x in "hl"] for u in range(2)]
    w2 = [[sb(f"w2{x}{u}", [P, EX_PAIRS, D], FP16) for x in "hl"] for u in range(2)]
    b1 = [sb(f"b1{u}", [P, 2 * EX_PAIRS], FP32) for u in range(2)]
    b2 = [sb(f"b2{u}", [P, D], FP32) for u in range(2)]
    xrow = {stage: sb(f"xrow{i}", [P, NBT, D], FP32) for i, stage in enumerate((shared, expert))}
    xh = sb("xh", [P, DT, NB], FP16)
    xl = sb("xl", [P, DT, NB], FP16)
    gel = sb("gel", [P, 2, NB], FP32)
    actf = sb("actf", [P, 2, NB], FP32)
    acth = sb("acth", [P, EX_PAIRS, NB], FP16)
    actl = sb("actl", [P, EX_PAIRS, NB], FP16)
    ysb = sb("ysb", [P, NBT, D], FP32)
    RING = 3 * QT
    yg = sb("yg", [P, RING, 2, D], FP32)

    def bank(name):
        return ctx.enter_context(nc.psum_tensor(f"ff_{name}", [P, 512], FP32))

    psH = [bank(f"psH{i}") for i in range(2)]
    psY = [bank(f"psY{i}") for i in range(2)]
    psX = bank("psX")
    psB = bank("psB")

    b_loaded, b_mm, b_ready = semaphore("b_loaded"), semaphore("b_mm"), semaphore("b_ready")
    link, cleared, zeroed = semaphore("link"), semaphore("cleared"), semaphore("zeroed")
    scattered, last_ready = semaphore("scattered"), semaphore("last_ready")
    table_ready, pos_ready, ratio_ready = semaphore("table_ready"), semaphore("pos_ready"), semaphore("ratio_ready")
    s_loaded, s_high, s_low = semaphore("s_loaded"), semaphore("s_high"), semaphore("s_low")
    w1_loaded, w2_loaded, b2_loaded = semaphore("w1_loaded"), semaphore("w2_loaded"), semaphore("b2_loaded")
    w_split = semaphore("w_split")
    alone = semaphore("alone")
    gathered = [semaphore(f"gathered{i}") for i in range(RING)]
    mixed, mix_link, stored = semaphore("mixed"), semaphore("mix_link"), semaphore("stored")
    xs, ys = scratch["xs"], scratch["ys"]
    out_v = io["out"].rearrange("b (t p) d -> p (b t) d", p=P)

    def of(stage, name, m, k=0):
        return stage.of(name, m, k)

    def table(eng, which, e, most):
        return eng.value_load(which[0:1, bass.ds(e, 1)], min_val=0, max_val=most)

    def experts(eng, before, body):
        eng.wait_ge(table_ready, 1)
        with eng.Fori(0, E // 2) as half:
            for u in range(2):
                e = half * 2 + u
                n = table(eng, blocks_i, e, N // NB)
                at = table(eng, first_i, e, NBLK - 1)
                if before:
                    before(e, u)

                def own(t):
                    with eng.If(t < n):
                        body(u, nc.s_assert_within(at + t, 0, NBLK - 1, skip_runtime_bounds_check_because=
                                                   "t < n, and an expert's last block is within all experts' blocks"))
                with eng.Fori(0, FEW) as t:
                    own(t)
                with eng.If(n > FEW):
                    with eng.Fori(FEW, N // NB) as t:
                        own(t)

    def shared_blocks(eng, body, lo, hi):
        with eng.Fori(lo, hi - 1) as m:
            body(m, True)
        body(hi - 1, False)

    def experts_done(eng, stage_name, extra=0):
        total = table(eng, first_i, E, NBLK)
        expert.until(eng, stage_name, of(expert, stage_name, total, extra), alone=True)

    shared_parts = [(s1[0][:, dt, :], s1[1][:, dt, :], st1[:, dt, 0:2 * HS]) for dt in range(DT)]
    shared_parts += [(s2[0][:], s2[1][:], st2[:, 0:SH_PAIRS, :])]
    block = ctx.enter_context(nc.Block())

    @block.sync
    def _(sp):
        sp.dma_start(st1[:, :, 0:2 * HS], io["Ws1"].rearrange("(t p) f -> p t f", p=P)).then_inc(s_loaded, 16)
        sp.dma_start(st2[:, 0:SH_PAIRS, :], io["Ws2"].rearrange("(t p) d -> p t d", p=P)).then_inc(s_loaded, 16)

        def until(stage, name, count):
            stage.until(sp, name, count, alone=True)

        def load_shared(m):
            until(shared, "xT_mm", of(shared, "xT_mm", m))
            sp.dma_start(xrow[shared][:], keep["xn2"][:, bass.ds(m * NBT, NBT), :]).then_inc(shared.sem["x_loaded"], 16)

        load_shared(0)
        sp.dma_start(b_raw[0:72, 0, :], io["be1"].rearrange("e (t p) -> (e t) p", p=P)[0:72, :]).then_inc(b_loaded, 16)
        sp.dma_start(b_raw[0:72, 1, :], io["be1"].rearrange("e (t p) -> (e t) p", p=P)[72:144, :]).then_inc(b_loaded, 16)
        sp.dma_start(b_raw[0:2 * SH_PAIRS, 2, :], io["bs1"].rearrange("(t p) -> t p", p=P)).then_inc(b_loaded, 16)
        sp.wait_ge(table_ready, 1)
        sp.wait_ge(cleared, 1)

        def zeros_after(e):
            end = table(sp, ends_i, e, X_ROWS - NB)
            sp.dma_start(xs[bass.ds(end, NB), :].rearrange("(j p) d -> p j d", p=P), zeros[:]).then_inc(zeroed, 16)

        with sp.Fori(0, E // 2) as m:
            load_shared(m + 1)
            zeros_after(m * 2)
            zeros_after(m * 2 + 1)
        for m in range(E // 2 + 1, FIRST_SHARED):
            load_shared(m)
        sp.dma_start(xs[E * REGION:, :].rearrange("(j p) d -> p j d", p=P), zeros[:]).then_inc(zeroed, 16)
        rest = ys[2 * N:, :].rearrange("(j p) d -> p j d", p=P)
        sp.dma_start(rest, zeros[:, 0:1, :].to_broadcast([P, (ROWS - 2 * N) // P, D])).then_inc(zeroed, 16)
        load_shared(FIRST_SHARED)
        sp.wait_ge(scattered, 2 * LEFT * QT * 16)
        sp.wait_ge(zeroed, (E + 2) * 16)

        def load_rows(n):
            until(expert, "xT_mm", of(expert, "xT_mm", n))
            row = table(sp, start_i, n, X_ROWS - NB)
            sp.dma_start(xrow[expert][:], xs[bass.ds(row, NB), :].rearrange("(j p) d -> p j d", p=P))\
                .then_inc(expert.sem["x_loaded"], 16)

        load_rows(0)

        def rows_of(u, n):
            load_rows(n + 1)
            until(expert, "y_stored", of(expert, "y_stored", n))
            until(expert, "y_ready", of(expert, "y_ready", n, 1))
            rows = ys[bass.ds(n * NB, NB), :].rearrange("(j p) d -> p j d", p=P)
            sp.dma_start(rows, ysb[:]).then_inc(expert.sem["y_stored"], 16)

        experts(sp, None, rows_of)

        def store_out(t):
            sp.wait_ge(mixed, t + QT)
            sp.dma_start(out_v[:, t:t + QT, :], keep["acc"][:, t:t + QT, :]).then_inc(stored, 16)

        for m in range(FIRST_SHARED + 1, N // NB):
            load_shared(m)
            if m >= FIRST_SHARED + 2:
                store_out((m - FIRST_SHARED - 2) * QT)
        for t in range(NT - 2 * QT, NT, QT):
            store_out(t)
        sp.wait_ge(stored, 16 * NT // QT)

    @block.gpsimd
    def _(pool):
        def wait_alone(sem, count):
            pool.wait_ge(sem, count)
            if not isinstance(count, int):
                pool.sem_inc(alone, 1)

        nc.gpsimd.memset(ones_e[:], 1.0)
        nc.gpsimd.memset(zeros[:], 0.0)
        nc.gpsimd.iota(number_i[:], pattern=[[1, NBLK + 1]], base=0, channel_multiplier=0).then_inc(cleared, 1)
        pool.wait_ge(last_ready, 1)
        for t in range(LEFT * QT):
            for k in range(2):
                pool.indirect_dma_start(out=xs[:, :], in_=keep["xn2"][:, NT - LEFT * QT + t, :], in_offset=None,
                                        out_offset=bass.IndirectOffsetOnAxis(ap=last_pos[:, k, t:t + 1], axis=0),
                                        bounds_check=X_ROWS - 1).then_inc(scattered, 16)

        def load_w1(e):
            pool.dma_start(st1[:], io["We1"][e].rearrange("(t p) f -> p t f", p=P)).then_inc(w1_loaded, 16)

        def load_w2(e, u):
            pool.dma_start(st2[:], io["We2"][e].rearrange("(t p) d -> p t d", p=P)).then_inc(w2_loaded, 16)

        PER = 2 * DT + 2

        def prepare(e, u, after):
            pool.dma_start(b2[u][:], io["be2"][e].partition_broadcast(P)).then_inc(b2_loaded, 16)
            wait_alone(w1_loaded, e * 16 + 16)
            for dt in range(DT):
                k = 2 * dt
                nc.gpsimd.tensor_scalar(w1[u][0][:, dt, :], st1[:, dt, :], 1.0, 0.0, ALU.mult, ALU.add).then_inc(w_split, 1)
                wait_alone(w_split, e * PER + k + 1)
                nc.gpsimd.tensor_tensor(w1[u][1][:, dt, :], st1[:, dt, :], w1[u][0][:, dt, :], ALU.subtract)\
                    .then_inc(w_split, 1)
            nc.gpsimd.tensor_copy(b1[u][:], b1T[:, bass.ds(e * 2 * EX_PAIRS, 2 * EX_PAIRS)])
            if after:
                wait_alone(w_split, e * PER + 2 * DT)
                load_w1(e + 1)
            wait_alone(w2_loaded, e * 16 + 16)
            flat = [x[:].rearrange("p t d -> p (t d)") for x in (st2, w2[u][0], w2[u][1])]
            nc.gpsimd.tensor_scalar(flat[1], flat[0], 1.0, 0.0, ALU.mult, ALU.add).then_inc(w_split, 1)
            wait_alone(w_split, e * PER + 2 * DT + 1)
            wait_alone(b2_loaded, e * 16 + 16)
            nc.gpsimd.tensor_tensor(flat[2], flat[0], flat[1], ALU.subtract).then_inc(w_split, 1)
            if after:
                wait_alone(w_split, (e + 1) * PER)
                load_w2(e + 1, u)

        pool.wait_ge(s_low, 3)
        load_w1(0)
        load_w2(0, 0)
        pool.wait_ge(b_ready, 3)
        prepare(0, 0, True)
        prepare(1, 1, True)
        pool.wait_ge(table_ready, 1)

        def used(e):
            done = table(pool, first_i, e - 1, NBLK)
            expert.until(pool, "y_ready", done, alone=True)

        with pool.Fori(1, E // 2 - 1) as half:
            for u in range(2):
                used(half * 2 + u)
                prepare(half * 2 + u, u, True)
        for u in range(2):
            used(E - 2 + u)
            prepare(E - 2 + u, u, u == 0)
        total = table(pool, first_i, E, NBLK)
        expert.until(pool, "y_stored", total * 16, alone=True)
        pool.wait_ge(pos_ready, 1)
        for t in range(NT):
            if t >= RING:
                pool.wait_ge(mixed, t - RING + 1)
            for k in range(2):
                pool.indirect_dma_start(out=yg[:, t % RING, k, :], out_offset=None, in_=ys[:, :],
                                        in_offset=bass.IndirectOffsetOnAxis(ap=pos[:, k, t:t + 1], axis=0),
                                        bounds_check=ROWS - 1).then_inc(gathered[t % RING], 16)

    @block.tensor
    def _(pe):
        pe.wait_ge(b_loaded, 48)
        for i, n in enumerate((72, 72, 2 * SH_PAIRS)):
            mm = nc.tensor.transpose(psB[:, 72 * i:72 * i + n], b_raw[0:n, i, :], keep["ident"][0:n, 0:n])
        mm.then_inc(b_mm, 1)

        def row_transposes(stage, m):
            stage.until(pe, "x_loaded", of(stage, "x_loaded", m, 16))
            stage.until(pe, "xl", of(stage, "xl", m))
            for dt in range(DT):
                for j in range(NBT):
                    mm = nc.tensor.transpose(psX[:, dt * NB + j * P:dt * NB + (j + 1) * P],
                                             xrow[stage][:, j, dt * P:(dt + 1) * P], keep["ident"][:])
            mm.then_inc(stage.sem["xT_mm"], 1)

        def ffn(stage, m, wa, wb, more):
            n = stage.pairs
            stage.until(pe, "xl", of(stage, "xl", m, 1))
            for j in range(n):
                stage.until(pe, "act", of(stage, "act", m, j - 1))
                for half in range(2):
                    lo = (half * n + j) * P
                    terms = [(wa[0], xh), (wa[0], xl), (wa[1], xh)]
                    for dt in range(DT):
                        for i, (a, x) in enumerate(terms):
                            mm = nc.tensor.matmul(psH[j % 2][:, half * NB:(half + 1) * NB], a[:, dt, lo:lo + P],
                                                  x[:, dt, :], start=(dt == 0 and i == 0), stop=(dt == DT - 1 and i == 2))
                mm.then_inc(stage.sem["h_mm"], 1)
            if more:
                row_transposes(stage, m + 1)
            stage.until(pe, "y_ready", of(stage, "y_ready", m))
            for j in range(n):
                stage.until(pe, "actl", of(stage, "actl", m, j + 1))
                for i in range(NBT):
                    terms = [(acth, wb[0]), (acth, wb[1]), (actl, wb[0])]
                    for s, (a, x) in enumerate(terms):
                        mm = nc.tensor.matmul(psY[i][:, 0:D], a[:, j, i * P:(i + 1) * P], x[:, j, :],
                                              start=(j == 0 and s == 0), stop=(j == n - 1 and s == 2))
            mm.then_inc(stage.sem["y_mm"], 1)

        row_transposes(shared, 0)
        pe.wait_ge(s_low, 3)

        def shared_block(m, more):
            ffn(shared, m, s1, s2, more)

        shared_blocks(pe, shared_block, 0, FIRST_SHARED)
        row_transposes(expert, 0)

        def weights_ready(e, u):
            pe.wait_ge(w_split, (e + 1) * (2 * DT + 2))
            pe.sem_inc(alone, 1)

        experts(pe, weights_ready, lambda u, n: ffn(expert, n, w1[u], w2[u], True))
        experts_done(pe, "xl", 1)
        row_transposes(shared, FIRST_SHARED)
        shared_blocks(pe, shared_block, FIRST_SHARED, N // NB)

    @block.scalar
    def _(act):
        act.wait_ge(s_loaded, 32)
        for hi, lo, src in shared_parts:
            nc.scalar.activation(hi, src, ACT.Copy).then_inc(s_high, 1)
        act.wait_ge(b_mm, 1)
        nc.scalar.activation(b1T[:], psB[:, 0:144], ACT.Copy).then_inc(b_ready, 1)
        nc.scalar.activation(bs1T[:], psB[:, 144:144 + 2 * SH_PAIRS], ACT.Copy).then_inc(b_ready, 1)
        nc.scalar.activation(ratio[:], keep["gap"][:], ACT.Exp, scale=1.0 / TAU).then_inc(ratio_ready, 1)
        act.wait_ge(b_ready, 2)
        act.sem_inc(b_ready, 1)

        def row_high(stage, m):
            stage.until(act, "xT_mm", of(stage, "xT_mm", m, 1))
            nc.scalar.activation(xh[:].rearrange("p t n -> p (t n)"), psX[:], ACT.Copy).then_inc(stage.sem["xh"], 1)

        def ffn(stage, m, bias, more):
            n = stage.pairs

            def high(j):
                stage.until(act, "act", of(stage, "act", m, j + 1))
                if j == 0:
                    stage.until(act, "y_mm", of(stage, "y_mm", m))
                nc.scalar.activation(acth[:, j, :], actf[:, j % 2, :], ACT.Copy).then_inc(stage.sem["acth"], 1)

            for j in range(n):
                stage.until(act, "act", of(stage, "act", m, j - 1))
                stage.until(act, "h_mm", of(stage, "h_mm", m, j + 1))
                nc.scalar.activation(gel[:, j % 2, :], psH[j % 2][:, NB:2 * NB], ACT.Gelu,
                                     bias=bias[:, n + j:n + j + 1]).then_inc(stage.sem["gelu"], 1)
                if j:
                    high(j - 1)
            high(n - 1)
            if more:
                row_high(stage, m + 1)

        row_high(shared, 0)

        def shared_block(m, more):
            ffn(shared, m, bs1T, more)

        shared_blocks(act, shared_block, 0, FIRST_SHARED)
        row_high(expert, 0)

        def biases_ready(e, u):
            act.wait_ge(w_split, (e + 1) * (2 * DT + 2))
            act.sem_inc(alone, 1)

        experts(act, biases_ready, lambda u, n: ffn(expert, n, b1[u], True))
        row_high(shared, FIRST_SHARED)
        shared_blocks(act, shared_block, FIRST_SHARED, N // NB)

    @block.vector
    def _(dve):
        steps = [0]

        def then(ins):
            steps[0] += 1
            ins.then_inc(link, 1)
            dve.wait_ge(link, steps[0])

        nc.vector.tensor_copy(last_pos[:], keep["row"][:, :, NT - LEFT * QT:NT]).then_inc(last_ready, 1)
        for i, (hi, lo, src) in enumerate(shared_parts):
            dve.wait_ge(s_high, i + 1)
            nc.vector.tensor_tensor(lo, src, hi, ALU.subtract).then_inc(s_low, 1)
        then(nc.vector.tensor_tensor(counts[:], keep["next_row"][:], keep["region"][:], ALU.subtract))
        nc.vector.tensor_copy(ends_i[:], keep["next_row"][:])
        then(nc.vector.tensor_scalar(counts_i[:], counts[:], float(NB - 1), None, ALU.add))
        then(nc.vector.tensor_scalar(blocks_i[:], counts_i[:], NB.bit_length() - 1, None, ALU.logical_shift_right))
        dve.wait_ge(cleared, 1)
        nc.vector.tensor_copy(number[:], number_i[:])
        then(nc.vector.tensor_copy(blocks[:], blocks_i[:]))
        then(nc.vector.tensor_tensor_scan(cum[:], ones_e[:], blocks[:], 0.0, ALU.mult, ALU.add))
        nc.vector.tensor_copy(first_i[:, E:E + 1], cum[:, E - 1:E])
        nc.vector.tensor_tensor(past[:], number[:].unsqueeze(2).to_broadcast([P, NBLK + 1, E]),
                                cum[:].unsqueeze(1).to_broadcast([P, NBLK + 1, E]), ALU.is_ge)
        nc.vector.tensor_scalar(beyond[:], blocks[:], float(-NB), float(REGION), ALU.mult, ALU.add)
        then(nc.vector.tensor_tensor(first[:], cum[:], blocks[:], ALU.subtract))
        nc.vector.tensor_copy(first_i[:, 0:E], first[:])
        then(nc.vector.tensor_tensor(past[:], past[:], beyond[:].unsqueeze(1).to_broadcast([P, NBLK + 1, E]), ALU.mult))
        then(nc.vector.tensor_reduce(start[:], past[:], AX.X, ALU.add))
        then(nc.vector.scalar_tensor_tensor(start[:], number[:], float(NB), start[:], ALU.mult, ALU.add))
        nc.vector.tensor_copy(start_i[:], start[:]).then_inc(table_ready, 1)
        then(nc.vector.scalar_tensor_tensor(shift[:], first[:], float(NB), keep["region"][:], ALU.mult, ALU.subtract))
        for k in range(2):
            ins = nc.vector.tensor_tensor(picked[:, k, :, :], keep["pick"][:, k, :, :],
                                          shift[:].unsqueeze(1).to_broadcast([P, NT, E]), ALU.mult)
        then(ins)
        then(nc.vector.tensor_reduce(posf[:].rearrange("p k t -> p (k t)"), picked[:].rearrange("p k t e -> p (k t) e"),
                                     AX.X, ALU.add))
        then(nc.vector.tensor_tensor(posf[:], posf[:], keep["row"][:], ALU.add))
        nc.vector.tensor_copy(pos[:], posf[:]).then_inc(pos_ready, 1)
        dve.wait_ge(ratio_ready, 1)
        then(nc.vector.tensor_scalar(denom[:], ratio[:], 1.0, None, ALU.add))
        then(nc.vector.reciprocal(w[0][:], denom[:]))
        then(nc.vector.tensor_tensor(w[1][:], ratio[:], w[0][:], ALU.mult))

        def row_low(stage, m):
            stage.until(dve, "xh", of(stage, "xh", m, 1))
            nc.vector.tensor_tensor(xl[:].rearrange("p t n -> p (t n)"), psX[:], xh[:].rearrange("p t n -> p (t n)"),
                                    ALU.subtract).then_inc(stage.sem["xl"], 1)

        def ffn(stage, m, bias, more, result, beside=None):
            n = stage.pairs

            def low(j):
                stage.until(dve, "acth", of(stage, "acth", m, j + 1))
                if j == 0:
                    stage.until(dve, "y_mm", of(stage, "y_mm", m))
                nc.vector.tensor_tensor(actl[:, j, :], actf[:, j % 2, :], acth[:, j, :], ALU.subtract)\
                    .then_inc(stage.sem["actl"], 1)

            for j in range(n):
                stage.until(dve, "actl", of(stage, "actl", m, j - 1))
                stage.until(dve, "gelu", of(stage, "gelu", m, j + 1))
                nc.vector.scalar_tensor_tensor(actf[:, j % 2, :], psH[j % 2][:, 0:NB], bias[:, j:j + 1],
                                               gel[:, j % 2, :], ALU.add, ALU.mult).then_inc(stage.sem["act"], 1)
                if j:
                    low(j - 1)
                if beside:
                    beside(j)
            low(n - 1)
            if more:
                row_low(stage, m + 1)
            stage.until(dve, "y_mm", of(stage, "y_mm", m, 1))
            result(m).then_inc(stage.sem["y_ready"], 1)

        def add_shared(m):
            for i in range(NBT):
                rows = keep["acc"][:, bass.ds(m * NBT + i, 1), :].rearrange("p o d -> p (o d)")
                ins = nc.vector.tensor_tensor(rows, psY[i][:, 0:D], rows, ALU.add)
            return ins

        row_low(shared, 0)
        shared_blocks(dve, lambda m, more: ffn(shared, m, bs1T, more, add_shared), 0, FIRST_SHARED)
        row_low(expert, 0)

        def expert_rows(u):
            def rows(n):
                expert.until(dve, "y_stored", of(expert, "y_stored", n))
                for i in range(NBT):
                    ins = nc.vector.tensor_tensor(ysb[:, i, :], psY[i][:, 0:D], b2[u][:], ALU.add)
                return ins
            return rows

        def biases_ready(e, u):
            dve.wait_ge(w_split, (e + 1) * (2 * DT + 2))
            dve.sem_inc(alone, 1)

        experts(dve, biases_ready, lambda u, n: ffn(expert, n, b1[u], True, expert_rows(u)))
        row_low(shared, FIRST_SHARED)

        def mix(t):
            rows = keep["acc"][:, t, :]
            dve.wait_ge(gathered[t % RING], 32 * (t // RING + 1))
            nc.vector.scalar_tensor_tensor(rows, yg[:, t % RING, 0, :], w[0][:, t:t + 1], rows, ALU.mult, ALU.add)\
                .then_inc(mix_link, 1)
            dve.wait_ge(mix_link, t + 1)
            nc.vector.scalar_tensor_tensor(rows, yg[:, t % RING, 1, :], w[1][:, t:t + 1], rows, ALU.mult, ALU.add)\
                .then_inc(mixed, 1)

        late = 2
        for m in range(FIRST_SHARED, N // NB):
            def beside(j):
                t = (m - FIRST_SHARED) * QT + j - late
                if t >= 0:
                    mix(t)
            if m > FIRST_SHARED:
                shared.until(dve, "y_ready", of(shared, "y_ready", m))
            ffn(shared, m, bs1T, m + 1 < N // NB, add_shared, beside)
        shared.until(dve, "y_ready", N // NB)
        for t in range(NT - late, NT):
            mix(t)

    ctx.close()



def xattn_moe(nc, io):
    ctx = ExitStack()
    with ctx:
        keep, scratch = keep_tensors(nc, ctx), scratch_tensors(nc)
        fast = Path(nc, ctx, "fast", [TK // KC - 1], 2, False)
        whole = Path(nc, ctx, "whole", list(range(TK // KC)), 1, True, before=fast)
        shared, expert = Stage(nc, ctx, "shared", SH_PAIRS), Stage(nc, ctx, "expert", EX_PAIRS)
        setup(nc, ctx, io, keep, scratch, [fast, shared, expert])
        attention(nc, fast, io, keep, scratch)
        odd = nc.values_load(keep["odd_i"][0:1, 0:1], min_val=0, max_val=P)
        with nc.If(odd > 0):
            attention(nc, whole, io, keep, scratch)
        feed_forward(nc, io, keep, scratch, shared, expert)


_INS = dict(x="x", ctx="ctx_1024", mask="mask_BxSxS2_bk1", Wq="L0_xattn_Wq", bq="L0_xattn_bq", Wk="L0_xattn_Wk",
            bk="L0_xattn_bk", Wv="L0_xattn_Wv", bv="L0_xattn_bv", Wo="L0_xattn_Wo", bo="L0_xattn_bo",
            Ws1="L0_ffn_Ws1", bs1="L0_ffn_bs1", Ws2="L0_ffn_Ws2", bs2="L0_ffn_bs2", We1="L0_ffn_We1",
            be1="L0_ffn_be1", We2="L0_ffn_We2", be2="L0_ffn_be2", Wr="L0_ffn_Wr", br="L0_ffn_br")


def kernel(**inputs):
    import numpy as _np
    import concourse.bacc as _bacc
    from concourse import mybir as _mybir
    from concourse.bass_utils import run_bass_kernel_spmd as _run

    nc = _bacc.Bacc("TRN2", target_bir_lowering=False, num_devices=1)
    arrays, io = {}, {}
    for short, name in _INS.items():
        a = _np.ascontiguousarray(inputs[name])
        arrays[f"in_{name}_dram"] = a
        io[short] = nc.dram_tensor(f"in_{name}_dram", a.shape, _mybir.dt.from_np(a.dtype), kind="ExternalInput").ap()
    io["out"] = nc.dram_tensor("out_0_dram", (B, TQ, D), FP32, kind="ExternalOutput").ap()
    xattn_moe(nc, io)
    r = _run(nc, [arrays], core_ids=[0])
    return r.results[0]["out_0_dram"]
```
